# Optimizing a Trainium2 kernel written in Bass

```python
import numpy as np
import jax
import jax.numpy as jnp

def _softmax(x, axis=-1):
    return jax.nn.softmax(x, axis=axis)

def _gelu(x):
    return jax.nn.gelu(x, approximate=True)

def _silu(x):
    return jax.nn.silu(x)

def _sigmoid(x):
    return jax.nn.sigmoid(x)

def _layernorm(x, axis=-1, eps=1e-05):
    m = jnp.mean(x, axis=axis, keepdims=True)
    v = jnp.var(x, axis=axis, keepdims=True)
    return (x - m) / jnp.sqrt(v + eps)

def _scatter_add(tgt, idx, src, axis=0):
    return tgt.at[idx].add(src)

def _segment_sum(src, seg, n):
    return jax.ops.segment_sum(src, seg, n)
kernel_name = 'mk_lm_tower_d1_tok_ids1024_r4_b146a3'

def setup_inputs(seed: int=0):
    np.random.seed(seed)
    _w = jnp.asarray

    def _rec_inputs():
        import jax
        import jax.numpy as jnp
        _rk = jax.random.key(seed)
        x = jax.random.randint(jax.random.fold_in(_rk, 1), (128, 128), 0, 30522, jnp.int32)
        mask_BS_i1_0 = jnp.where(jnp.ones((128, 128), dtype=bool), 1, 0).astype(jnp.int32)
        return (x, mask_BS_i1_0)
    x, mask_BS_i1_0 = _rec_inputs()

    def _L0_tok_setup():
        import jax, jax.numpy as jnp
        import numpy as np
        VOCAB = 30522
        HIDDEN = 256
        MAX_POS = 128
        TYPE_VOCAB = 2
        EPS = 1e-12
        key = jax.random.key(seed)
        k1, k2, k3, k4, k5 = jax.random.split(key, 5)
        B, S = (128, 128)
        input_ids = jax.random.randint(k1, (B, S), 0, VOCAB, dtype=jnp.int64)
        token_type_ids = jax.random.randint(k2, (B, S), 0, TYPE_VOCAB, dtype=jnp.int64)
        word_emb = jax.random.normal(k3, (VOCAB, HIDDEN), dtype=jnp.float32) * 0.02
        word_emb = word_emb.at[0].set(0.0)
        pos_emb = jax.random.normal(k4, (MAX_POS, HIDDEN), dtype=jnp.float32) * 0.02
        type_emb = jax.random.normal(k5, (TYPE_VOCAB, HIDDEN), dtype=jnp.float32) * 0.02
        gamma = jnp.ones((HIDDEN,), dtype=jnp.float32)
        beta = jnp.zeros((HIDDEN,), dtype=jnp.float32)
        return {'input_ids': input_ids, 'token_type_ids': token_type_ids, 'word_emb': word_emb, 'pos_emb': pos_emb, 'type_emb': type_emb, 'gamma': gamma, 'beta': beta}
    _L0_tok_all = _L0_tok_setup()
    _L0_tok_in = {k: v for k, v in _L0_tok_all.items() if k in ('word_emb', 'pos_emb', 'type_emb', 'gamma', 'beta')}
    del _L0_tok_all

    def _L0_attn_setup():
        import jax, jax.numpy as jnp
        import numpy as np
        N_HEADS = 16
        MAX_DIST = 64
        key = jax.random.key(seed)
        ks = jax.random.split(key, 7)
        B, S, D = (16, 128, 256)
        hd = D // N_HEADS
        num_rel = 2 * MAX_DIST + 1
        s = 0.02
        return {'x': jax.random.normal(ks[0], (B, S, D), dtype=jnp.float32), 'Wq': jax.random.normal(ks[1], (D, D), dtype=jnp.float32) * s, 'Wk': jax.random.normal(ks[2], (D, D), dtype=jnp.float32) * s, 'Wv': jax.random.normal(ks[3], (D, D), dtype=jnp.float32) * s, 'Eq': jax.random.normal(ks[4], (num_rel, hd), dtype=jnp.float32) * s, 'Ek': jax.random.normal(ks[5], (num_rel, hd), dtype=jnp.float32) * s, 'Ev': jax.random.normal(ks[6], (num_rel, hd), dtype=jnp.float32) * s}
    _L0_attn_all = _L0_attn_setup()
    _L0_attn_in = {k: v for k, v in _L0_attn_all.items() if k in ('Wq', 'Wk', 'Wv', 'Eq', 'Ek', 'Ev')}
    del _L0_attn_all

    def _L0_ffn_setup():
        import jax, jax.numpy as jnp
        import numpy as np
        DIM = 256

        def _reference_tuple_inner(x, W_r, W_k, W_v, mu_r, mu_k):
            B, T, C = x.shape
            x_prev = jnp.concatenate([jnp.zeros((B, 1, C), x.dtype), x[:, :-1, :]], axis=1)
            xr = mu_r * x + (1.0 - mu_r) * x_prev
            xk = mu_k * x + (1.0 - mu_k) * x_prev
            r = jax.nn.sigmoid(jnp.einsum('btc,dc->btd', xr, W_r))
            k = jnp.einsum('btc,dc->btd', xk, W_k)
            k_act = jnp.square(jax.nn.relu(k))
            out = r * jnp.einsum('btc,dc->btd', k_act, W_v)
            new_state = x[:, -1, :]
            return (out, new_state)
        key = jax.random.key(seed)
        ks = jax.random.split(key, 6)
        B, T, C = (8, 512, DIM)
        x = jax.random.normal(ks[0], (B, T, C), dtype=jnp.float32)
        s = 1.0 / np.sqrt(C)
        W_r = jax.random.uniform(ks[1], (C, C), jnp.float32, -s, s)
        W_k = jax.random.uniform(ks[2], (C, C), jnp.float32, -s, s)
        W_v = jax.random.uniform(ks[3], (C, C), jnp.float32, -s, s)
        mu_r = jax.random.uniform(ks[4], (C,), jnp.float32)
        mu_k = jax.random.uniform(ks[5], (C,), jnp.float32)
        return {'x': x, 'W_r': W_r, 'W_k': W_k, 'W_v': W_v, 'mu_r': mu_r, 'mu_k': mu_k}
    _L0_ffn_all = _L0_ffn_setup()
    _L0_ffn_in = {k: v for k, v in _L0_ffn_all.items() if k in ('W_r', 'W_k', 'W_v', 'mu_r', 'mu_k')}
    del _L0_ffn_all
    return {'x': x, 'mask_BS_i1_0': mask_BS_i1_0, 'L0_tok_word_emb': _L0_tok_in['word_emb'], 'L0_tok_pos_emb': _L0_tok_in['pos_emb'], 'L0_tok_type_emb': _L0_tok_in['type_emb'], 'L0_tok_gamma': _L0_tok_in['gamma'], 'L0_tok_beta': _L0_tok_in['beta'], 'L0_attn_Wq': _L0_attn_in['Wq'], 'L0_attn_Wk': _L0_attn_in['Wk'], 'L0_attn_Wv': _L0_attn_in['Wv'], 'L0_attn_Eq': _L0_attn_in['Eq'], 'L0_attn_Ek': _L0_attn_in['Ek'], 'L0_attn_Ev': _L0_attn_in['Ev'], 'L0_ffn_W_r': _L0_ffn_in['W_r'], 'L0_ffn_W_k': _L0_ffn_in['W_k'], 'L0_ffn_W_v': _L0_ffn_in['W_v'], 'L0_ffn_mu_r': _L0_ffn_in['mu_r'], 'L0_ffn_mu_k': _L0_ffn_in['mu_k']}

def reference(x, mask_BS_i1_0, L0_tok_word_emb, L0_tok_pos_emb, L0_tok_type_emb, L0_tok_gamma, L0_tok_beta, L0_attn_Wq, L0_attn_Wk, L0_attn_Wv, L0_attn_Eq, L0_attn_Ek, L0_attn_Ev, L0_ffn_W_r, L0_ffn_W_k, L0_ffn_W_v, L0_ffn_mu_r, L0_ffn_mu_k):
    import jax
    import jax.numpy as jnp

    def _L0_tok_ref(input_ids, token_type_ids, word_emb, pos_emb, type_emb, gamma, beta):
        import jax, jax.numpy as jnp
        import numpy as np
        VOCAB = 30522
        HIDDEN = 256
        MAX_POS = 128
        TYPE_VOCAB = 2
        EPS = 1e-12
        B, S = input_ids.shape
        pos = pos_emb[:S][None, :, :]
        x = word_emb[input_ids] + pos + type_emb[token_type_ids]
        mu = jnp.mean(x, axis=-1, keepdims=True)
        var = jnp.mean(jnp.square(x - mu), axis=-1, keepdims=True)
        y = (x - mu) * jax.lax.rsqrt(var + EPS) * gamma + beta
        return y

    def _L0_attn_ref(x, Wq, Wk, Wv, Eq, Ek, Ev):
        import jax, jax.numpy as jnp
        import numpy as np
        N_HEADS = 16
        MAX_DIST = 64
        B, S, D = x.shape
        H = N_HEADS
        hd = D // H
        r = jnp.arange(S)
        rel = jnp.clip(r[:, None] - r[None, :], -MAX_DIST, MAX_DIST) + MAX_DIST

        def proj(W):
            return jnp.einsum('bsd,de->bse', x, W).reshape(B, S, H, hd).transpose(0, 2, 1, 3)
        q, k, v = (proj(Wq), proj(Wk), proj(Wv))
        a_q = Eq[rel]
        a_k = Ek[rel]
        a_v = Ev[rel]
        content = jnp.einsum('bhld,bhmd->bhlm', q, k)
        rel_k = jnp.einsum('bhld,lmd->bhlm', q, a_k)
        rel_q = jnp.einsum('bhmd,lmd->bhlm', k, a_q)
        pos_pos = jnp.einsum('lmd,lmd->lm', a_q, a_k)
        scale = 1.0 / hd ** 0.5
        logits = (content + rel_k + rel_q + pos_pos) * scale
        attn = jax.nn.softmax(logits, axis=-1)
        out = jnp.einsum('bhlm,bhmd->bhld', attn, v) + jnp.einsum('bhlm,lmd->bhld', attn, a_v)
        return out.transpose(0, 2, 1, 3).reshape(B, S, D)

    def _L0_ffn_ref(x, W_r, W_k, W_v, mu_r, mu_k):
        import jax, jax.numpy as jnp
        import numpy as np
        DIM = 256

        def _reference_tuple_inner(x, W_r, W_k, W_v, mu_r, mu_k):
            B, T, C = x.shape
            x_prev = jnp.concatenate([jnp.zeros((B, 1, C), x.dtype), x[:, :-1, :]], axis=1)
            xr = mu_r * x + (1.0 - mu_r) * x_prev
            xk = mu_k * x + (1.0 - mu_k) * x_prev
            r = jax.nn.sigmoid(jnp.einsum('btc,dc->btd', xr, W_r))
            k = jnp.einsum('btc,dc->btd', xk, W_k)
            k_act = jnp.square(jax.nn.relu(k))
            out = r * jnp.einsum('btc,dc->btd', k_act, W_v)
            new_state = x[:, -1, :]
            return (out, new_state)
        return _reference_tuple_inner(x, W_r, W_k, W_v, mu_r, mu_k)[0]
    h = _L0_tok_ref(x, mask_BS_i1_0, L0_tok_word_emb, L0_tok_pos_emb, L0_tok_type_emb, L0_tok_gamma, L0_tok_beta)
    h = h + _L0_attn_ref(_layernorm(h, axis=-1), L0_attn_Wq, L0_attn_Wk, L0_attn_Wv, L0_attn_Eq, L0_attn_Ek, L0_attn_Ev)
    h = h + _L0_ffn_ref(_layernorm(h, axis=-1), L0_ffn_W_r, L0_ffn_W_k, L0_ffn_W_v, L0_ffn_mu_r, L0_ffn_mu_k)
    return h

_drawn_inputs = setup_inputs


def setup_inputs(seed=0):
    import zlib

    import numpy as np

    out = dict(_drawn_inputs(seed))
    spreads = {'L0_tok_gamma': (1.0, 0.2), 'L0_tok_beta': (0.0, 0.1)}
    factors = {'L0_attn_Wq': 8.0,
     'L0_attn_Wk': 8.0,
     'L0_attn_Eq': 8.0,
     'L0_attn_Ek': 8.0,
     'L0_attn_Ev': 8.0,
     'L0_ffn_mu_r': 6.897}
    for name, (base, spread) in spreads.items():
        noise = np.random.default_rng([zlib.crc32(name.encode()), seed]).standard_normal(out[name].shape)
        drawn = base * np.exp(spread * noise) if base else spread * noise
        out[name] = jnp.asarray(drawn.astype(out[name].dtype))
    for name, factor in factors.items():
        out[name] = (out[name] * factor).astype(out[name].dtype)
    return out
```

```python
import concourse.bass as bass
from concourse import mybir
from contextlib import ExitStack

fp32 = mybir.dt.float32
bf16 = mybir.dt.bfloat16
i32 = mybir.dt.int32
ALU = mybir.AluOpType
ACT = mybir.ActivationFunctionType

P = 128
B, S, D = 128, 128, 256
H, HD = 16, 16
R = 64
GB = 4
NG = B // GB
TOK = GB * S
HB = H * GB
CT = D // P
NPART = 3
SLOTS = 6
TW = 2 * S - 1
VW = HD + 1
Q_PART = (0, 0, 0, 1, 1, 2)
K_PART = (0, 1, 2, 0, 1, 0)
KR = SLOTS * HD
KR1 = KR + NPART
RC = 8
NRC = S // RC
LAG = 4
SCALE = 1.0 / HD ** 0.5
LOWEST = -3.4028234e38
EPS_EMBED, EPS_NORM = 1e-12, 1e-5


def tower_kernel(nc, ids, types, word, pos, typ, gamma, beta, wq, wk, wv, eq, ek, ev,
                 wr_t, wk_t, wv_t, mu_r, mu_k, out):
    ctx = ExitStack()
    with ctx:
        def sb(name, shape, dt=fp32):
            return ctx.enter_context(nc.sbuf_tensor(name, shape, dt))

        def sem(name):
            return ctx.enter_context(nc.semaphore(name))

        rk = sb("rk", [P, HB * S])
        rq = sb("rq", [P, HB * S])
        qs = [sb(f"qs{i}", [P, HB * S], bf16) for i in range(2)]
        ks = [sb(f"ks{i}", [P, HB * S], bf16) for i in range(2)]
        vx = [sb(f"vx{i}", [P, GB * H * VW]) for i in range(2)]
        h = [sb(f"h{i}", [P, GB * D]) for i in range(2)]
        norm = sb("norm", [P, GB * D])
        normT = sb("normT", [P, CT * GB * (S + 1)])
        qparts = sb("qparts", [P, NPART * CT * TOK], bf16)
        kparts = sb("kparts", [P, NPART * CT * TOK], bf16)
        pv = [sb(f"pv{i}", [P, TOK]) for i in range(2)]
        ot = sb("ot", [P, HB * VW])
        orel = sb("orel", [P, HD * HB])
        xr = sb("xr", [P, CT * TOK])
        xk = sb("xk", [P, CT * TOK])
        kact = xr
        avt = sb("avt", [P, S * HD])
        ekw = sb("ekw", [P, TW], bf16)
        eqw = sb("eqw", [P, TW], bf16)
        w_q, w_k, w_v, w_r, w_fk, w_fv = (sb(n, [P, CT * D]) for n in
                                          ("w_q", "w_k", "w_v", "w_r", "w_fk", "w_fv"))
        ident = sb("ident", [P, P])
        pos0 = sb("pos0", [P, D])
        dtype_ = sb("dtype_", [P, D])
        gam = sb("gam", [P, D])
        bet = sb("bet", [P, D])
        mur = sb("mur", [P, CT])
        muk = sb("muk", [P, CT])
        neghalf = sb("neghalf", [P, GB])
        idt = sb("idt", [P, GB], i32)
        tyt = sb("tyt", [P, GB], i32)
        tyf = sb("tyf", [P, GB])
        bn = [sb(f"bn{i}", [P, GB * 6]) for i in range(3)]
        mv = [sb(f"mv{i}", [P, GB * 2]) for i in range(3)]
        rstd = [sb(f"rstd{i}", [P, GB]) for i in range(3)]
        mx = sb("mx", [P, HB])
        rden = sb("rden", [P, HB])
        ekf = rk[0:HD, 0:TW]
        ekr = rk[0:HD, TW:2 * TW]
        eqf = rk[0:HD, 2 * TW:3 * TW]
        prod = rk[0:HD, 3 * TW:4 * TW]
        rest = rk[0:HD, 4 * TW:5 * TW]
        ones = rk[0:HD, 5 * TW:5 * TW + 1]
        pp = rk[0:1, 6 * TW:7 * TW]
        k_tab = qs[0][0:HD, 0:NPART * TW]
        q_tab = qs[1][0:HD, 0:NPART * TW]
        pp_tab = ks[0][0:1, 0:NPART * TW]

        ps = [ctx.enter_context(nc.psum_tensor(f"ps{i}", [P, 512], fp32)) for i in range(8)]

        ev_wide = nc.dram_tensor("ev_wide", [TW, HD], fp32, kind="Internal")
        q_dram = nc.dram_tensor("q_dram", [NPART, D, TOK], bf16, kind="Internal").ap()
        k_dram = nc.dram_tensor("k_dram", [NPART, D, TOK], bf16, kind="Internal").ap()
        o_dram = nc.dram_tensor("o_dram", [HD, S, HB], fp32, kind="Internal").ap()

        rk3 = rk[:, :].rearrange("p (n l) -> p n l", l=S)
        rq3 = rq[:, :].rearrange("p (n m) -> p n m", m=S)
        qs3 = [t[:, :].rearrange("p (n l) -> p n l", l=S) for t in qs]
        ks3 = [t[:, :].rearrange("p (n l) -> p n l", l=S) for t in ks]
        vx4 = [t[:, :].rearrange("p (b h c) -> p b h c", b=GB, c=VW) for t in vx]
        nT = normT[:, :].rearrange("p (n s) -> p n s", s=S + 1)
        qp = qparts[:, :].rearrange("p (k t) -> p k t", k=NPART)
        kp = kparts[:, :].rearrange("p (k t) -> p k t", k=NPART)
        ot3 = ot[:, :].rearrange("p (n c) -> p n c", c=VW)
        ot4 = ot[:, :].rearrange("p (b h c) -> p b h c", b=GB, c=VW)
        oav = rq[:, 0:S // 4 * HB]

        const_in = sem("const_in")
        setup_v = sem("setup_v")
        setup_g = sem("setup_g")
        pp_sum = sem("pp_sum")
        slots_in = sem("slots_in")
        wide_out = sem("wide_out")
        full = [sem(f"full{i}") for i in range(6)]
        empty = [sem(f"empty{i}") for i in range(6)]
        full_e = [sem(f"full_e{i}") for i in range(2)]
        empty_e = [sem(f"empty_e{i}") for i in range(2)]
        full_m = [sem(f"full_m{i}") for i in range(2)]
        empty_m = [sem(f"empty_m{i}") for i in range(2)]
        ids_in = sem("ids_in")
        words_in = sem("words_in")
        pos_added = sem("pos_added")
        tyf_ready = sem("tyf_ready")
        x_ready = sem("x_ready")
        stats = [sem(f"stats{i}") for i in range(3)]
        meanvar = [sem(f"meanvar{i}") for i in range(3)]
        eps_added = [sem(f"eps_added{i}") for i in range(3)]
        rstd_ready = [sem(f"rstd_ready{i}") for i in range(3)]
        normed = [sem(f"normed{i}") for i in range(3)]
        scaled = sem("scaled")
        h_ready = sem("h_ready")
        part0 = sem("part0")
        part1 = sem("part1")
        part2 = sem("part2")
        q_out = sem("q_out")
        k_out = sem("k_out")
        q_in = sem("q_in")
        k_in = sem("k_in")
        centred = sem("centred")
        exp_done = sem("exp_done")
        oav_out = sem("oav_out")
        orel_in = sem("orel_in")
        rden_ready = sem("rden_ready")
        o_sum = sem("o_sum")
        o_norm = sem("o_norm")
        h2_ready = sem("h2_ready")
        diff_ready = sem("diff_ready")
        mixed = sem("mixed")
        squared = sem("squared")
        gated = sem("gated")
        result = sem("result")
        stored = sem("stored")
        passed = sem("passed")

        N_CONST = 16 * (6 + 5 + 2 + 2 + 1)
        N_SETUP_G = 4 + 2
        N_SETUP_V = 4 + 3 + 3 * 5 + 1 + 2 + 2
        EPS = (EPS_EMBED, EPS_NORM, EPS_NORM)

        USES = (10, 10, 16, 16, 12, 12)

        def rk_bank(c):
            return (0, 2)[c % 2]

        def rq_bank(c):
            return (1, 3)[c % 2]

        def n_rel(g, bank, c):
            return g * USES[bank] + c // 2

        def n_logit(g, u):
            return g * USES[2 + u % 2] + NRC // 2 + u // 2

        def n_av(g, c):
            return g * USES[c % 2] + NRC // 2 + c // 2

        def n_probT(g, u):
            return g * USES[4] + 3 * (u // 4) + u % 4 // 2

        def n_pv(g, q):
            return g * USES[4] + 3 * q + 2

        def past(g, n=1):
            return not isinstance(g, int) or g >= n

        def apart(eng):
            eng.sem_inc(passed, 1)

        def order(attend, mix, embed):
            steps = []
            m_steps = [("combine",), ("norm2",), ("transpose2",), ("shift",), ("gates",), ("keys",)] if mix else []
            at = {1: 0, 3: 1, 6: 2, 8: 3, 11: 4, 13: 5}
            if attend:
                for c in range(NRC):
                    if c in at and m_steps:
                        steps.append(m_steps[at[c]])
                    steps.append(("relative", c))
            else:
                steps += m_steps
            if mix:
                steps.append(("values",))
            e_steps = [("fetch",), ("gather",), ("embed",), ("norm1",), ("transpose1",), ("project_q",),
                       ("project_k",), ("project_v",)] if embed else []
            at = {0: 0, 1: 1, 3: 2, 5: 3, 7: 4, 8: 5, 10: 6, 13: 7}
            if attend:
                for u in range(H + LAG):
                    if u in at and e_steps:
                        steps.append(e_steps[at[u]])
                    if u < H:
                        steps.append(("logits", u))
                    if u >= LAG:
                        steps.append(("probT", u - LAG))
                        if (u - LAG) % 4 == 0 and u > LAG:
                            steps.append(("turn", (u - LAG) // 4 - 1))
                        if (u - LAG) % 4 == 3:
                            steps.append(("weigh", (u - LAG) // 4))
                for c in range(4):
                    steps.append(("weigh_rel", c))
                    if c == 0:
                        steps.append(("turn", H // 4 - 1))
                steps.append(("store_rel",))
            else:
                steps += e_steps
            return steps

        MIX = ("combine", "norm2", "transpose2", "shift", "gates", "keys", "values")
        EMBED = ("fetch", "gather", "embed", "norm1", "transpose1", "project_q", "project_k", "project_v")

        def run(steps, table, g, par):
            for name, *arg in steps:
                if name in table:
                    d = -1 if name in MIX else 1 if name in EMBED else 0
                    table[name](g + d, (par + d) % 2, *arg)

        def pipeline(eng, table):
            run(order(False, False, True), table, -1, 1)
            run(order(True, False, True), table, 0, 0)
            with eng.Fori(0, NG // 2 - 1) as t:
                for i in (1, 2):
                    run(order(True, True, True), table, t * 2 + i, i % 2)
            run(order(True, True, False), table, NG - 1, 1)
            run(order(False, True, False), table, NG, 0)

        def embeds_before_mix(g):
            return min(g + 2, NG) if isinstance(g, int) else g + 2

        block = ctx.enter_context(nc.Block())

        @block.sync
        def _(sp):
            def load(dst, src):
                sp.dma_start(dst, src).then_inc(const_in, 16)

            for dst, src in ((w_q, wq), (w_k, wk), (w_v, wv), (w_r, wr_t), (w_fk, wk_t), (w_fv, wv_t)):
                load(dst[:, :].rearrange("p (c n) -> p c n", c=CT), src.rearrange("(c p) n -> p c n", p=P))
            load(pos0[:, :], pos)
            load(gam[:, :], bass.AP(gamma.tensor, 0, [[0, P], [1, D]]))
            load(bet[:, :], bass.AP(beta.tensor, 0, [[0, P], [1, D]]))
            load(mur[:, :], mu_r)
            load(muk[:, :], mu_k)
            load(norm[:, 0:D], bass.AP(typ.tensor, 0, [[0, P], [1, D]]))
            load(norm[:, D:2 * D], bass.AP(typ.tensor, D, [[0, P], [1, D]]))
            load(ekf[:, R - 1:3 * R], ek)
            load(eqf[:, R - 1:3 * R], eq)
            wide = ev_wide.ap()
            sp.dma_start(wide[0:R - 1, :], bass.AP(ev.tensor, 0, [[0, R - 1], [1, HD]])).then_inc(wide_out, 16)
            sp.dma_start(wide[R - 1:3 * R, :], ev).then_inc(wide_out, 16)
            sp.dma_start(wide[3 * R:TW, :], bass.AP(ev.tensor, 2 * R * HD, [[0, R - 1], [1, HD]])).then_inc(wide_out, 16)
            sp.wait_ge(wide_out, 48)
            load(avt[:, :], bass.AP(ev_wide, 0, [[HD, P], [1, S * HD]]))
            sp.wait_ge(setup_v, N_SETUP_V)
            for s in range(SLOTS):
                sp.dma_start(ekw[s * HD:(s + 1) * HD, :], k_tab[:, K_PART[s] * TW:(K_PART[s] + 1) * TW]).then_inc(slots_in, 16)
                sp.dma_start(eqw[s * HD:(s + 1) * HD, :], q_tab[:, Q_PART[s] * TW:(Q_PART[s] + 1) * TW]).then_inc(slots_in, 16)
            for s in range(NPART):
                sp.dma_start(eqw[KR + s:KR + s + 1, :], pp_tab[:, s * TW:(s + 1) * TW]).then_inc(slots_in, 16)
            sp.wait_ge(slots_in, 16 * (2 * SLOTS + NPART))

            def fetch(g, par):
                if past(g):
                    sp.wait_ge(words_in, 16 * GB * g)
                if past(g):
                    sp.wait_ge(tyf_ready, g)
                    apart(sp)
                sp.dma_start(idt[:, :], ids[g]).then_inc(ids_in, 16)
                sp.dma_start(tyt[:, :], types[g]).then_inc(ids_in, 16)

            def parts_through_dram(g, parts, dram, slots, part_of, n_parts, out_done, in_done):
                if past(g):
                    sp.wait_ge(in_done, 16 * SLOTS * g)
                    apart(sp)
                sp.wait_ge(part2, n_parts)
                for n in range(NPART):
                    sp.dma_start(dram[n].rearrange("(c p) t -> p c t", p=P),
                                 parts[:, n, :].rearrange("p (c t) -> p c t", c=CT)).then_inc(out_done, 16)
                sp.wait_ge(out_done, 16 * NPART * (g + 1))
                for s in range(SLOTS):
                    sp.dma_start(slots[s * HD:(s + 1) * HD, :].rearrange("p (n t) -> p n t", t=TOK),
                                 dram[part_of[s]].rearrange("(n d) t -> d n t", d=HD)).then_inc(in_done, 16)

            def project_q(g, par):
                parts_through_dram(g, qp, q_dram, qs[par], Q_PART, 4 * g + 2, q_out, q_in)

            def project_k(g, par):
                parts_through_dram(g, kp, k_dram, ks[par], K_PART, 4 * g + 4, k_out, k_in)

            def store_rel(g, par):
                if past(g):
                    sp.wait_ge(orel_in, 16 * g)
                    apart(sp)
                for n in range(2):
                    sp.wait_ge(empty[n], (g + 1) * USES[n])
                    apart(sp)
                for j in range(4):
                    sp.dma_start(o_dram[:, 32 * j:32 * j + 32, :].rearrange("d l n -> d (l n)"),
                                 oav[32 * j:32 * j + HD, :]).then_inc(oav_out, 16)
                sp.wait_ge(oav_out, 64 * (g + 1))
                if past(g):
                    sp.wait_ge(o_sum, g)
                    apart(sp)
                sp.dma_start(orel[:, :].rearrange("p (d n) -> p d n", n=HB),
                             o_dram.rearrange("d l n -> l d n")).then_inc(orel_in, 16)

            def values(g, par):
                sp.wait_ge(result, 2 * (g + 1))
                apart(sp)
                sp.dma_start(out[g], h[par][:, :].rearrange("p (b n) -> p b n", b=GB)).then_inc(stored, 16)

            pipeline(sp, dict(fetch=fetch, project_q=project_q, project_k=project_k, store_rel=store_rel,
                              values=values))
            sp.wait_ge(stored, 16 * NG)

        @block.gpsimd
        def _(pool):
            gps = nc.gpsimd
            gps.memset(ident[:, :], 0.0).then_inc(setup_g, 1)
            pool.wait_ge(setup_g, 1)
            gps.affine_select(out=ident[:, :], in_=ident[:, :], compare_op=ALU.not_equal, fill=1.0, base=0,
                              pattern=[[-1, P]], channel_multiplier=1).then_inc(setup_g, 1)
            gps.memset(neghalf[:, :], -0.5).then_inc(setup_g, 1)
            gps.memset(normT[:, :], 0.0).then_inc(setup_g, 1)
            for i in range(2):
                gps.memset(vx[i][:, :], 1.0).then_inc(setup_g, 1)
            pool.wait_ge(setup_g, N_SETUP_G)
            pool.wait_ge(const_in, N_CONST)
            pool.wait_ge(setup_v, N_SETUP_V)

            def inverse_root(kind, g):
                pool.wait_ge(meanvar[kind], GB * (g + 1))
                apart(pool)
                gps.tensor_scalar(rstd[kind][:, :], mv[kind][:, 1::2], EPS[kind], None, ALU.add).then_inc(eps_added[kind], 1)
                pool.wait_ge(eps_added[kind], g + 1)
                gps.tensor_tensor(rstd[kind][:, :], rstd[kind][:, :], neghalf[:, :], ALU.pow).then_inc(rstd_ready[kind], 1)

            def gather(g, par):
                pool.wait_ge(ids_in, 32 * (g + 1))
                if past(g, 2):
                    pool.wait_ge(stored, 16 * (g - 1))
                    apart(pool)
                for b in range(GB):
                    gps.indirect_dma_start(h[par][:, b * D:(b + 1) * D], None, word,
                                           bass.IndirectOffsetOnAxis(ap=idt[:, b:b + 1], axis=0)).then_inc(words_in, 16)

            def embed(g, par):
                pool.wait_ge(words_in, 16 * GB * (g + 1))
                h3 = h[par][:, :].rearrange("p (b n) -> p b n", b=GB)
                gps.tensor_tensor(h3, h3, pos0[:, :].unsqueeze(1).broadcast_to([P, GB, D]), ALU.add).then_inc(pos_added, 1)
                inverse_root(0, g)
                pool.wait_ge(normed[0], GB * (g + 1))
                gps.tensor_tensor(h3, h3, gam[:, :].unsqueeze(1).broadcast_to([P, GB, D]), ALU.mult).then_inc(scaled, 1)
                pool.wait_ge(scaled, g + 1)
                gps.tensor_tensor(h3, h3, bet[:, :].unsqueeze(1).broadcast_to([P, GB, D]), ALU.add).then_inc(h_ready, 1)

            def norm1(g, par):
                inverse_root(1, g)

            def logits(g, par, u):
                pool.wait_ge(empty[2 + u % 2], n_logit(g, u) + 1)
                part = rq3[:, GB * u:GB * (u + 1), :]
                gps.tensor_tensor(part, part, mx[:, GB * u:GB * (u + 1)].unsqueeze(2).broadcast_to([P, GB, S]),
                                  ALU.subtract).then_inc(centred, 1)

            def combine(g, par):
                pool.wait_ge(o_norm, g + 1)
                gps.tensor_tensor(h[par][:, :], h[par][:, :], norm[:, :], ALU.add).then_inc(h2_ready, 1)

            def norm2(g, par):
                inverse_root(2, g)

            def keys(g, par):
                for e in range(CT):
                    pool.wait_ge(empty_m[e], 4 * g + 3)
                    t = kact[:, e * TOK:(e + 1) * TOK]
                    gps.tensor_tensor(t, t, t, ALU.mult).then_inc(squared, 1)

            pipeline(pool, dict(gather=gather, embed=embed, norm1=norm1, logits=logits, combine=combine,
                                norm2=norm2, keys=keys))

        @block.scalar
        def _(act):
            act.wait_ge(setup_g, N_SETUP_G)

            def copy(dst, src):
                return nc.scalar.activation(dst, src, ACT.Copy)

            def transpose1(g, par):
                for c in range(CT):
                    act.wait_ge(full_e[c], 4 * g + 1)
                    copy(nT[:, c * GB:(c + 1) * GB, 1:S + 1],
                         ps[6 + c][:, :].rearrange("p (b s) -> p b s", b=GB)).then_inc(empty_e[c], 1)

            def split(g, n, use, parts, out_done):
                if past(g):
                    act.wait_ge(out_done, 16 * NPART * g)
                for e in range(CT):
                    act.wait_ge(full_e[e], 4 * g + use + 1)
                    copy(parts[:, 0, e * TOK:(e + 1) * TOK], ps[6 + e][:, :]).then_inc(part0, 1)
                for e in range(CT):
                    act.wait_ge(empty_e[e], 4 * g + use + 1)
                    copy(parts[:, 1, e * TOK:(e + 1) * TOK], norm[:, e * TOK:(e + 1) * TOK]).then_inc(part1, 1)

            def project_q(g, par):
                split(g, 0, 1, qp, q_out)

            def project_k(g, par):
                split(g, 1, 2, kp, k_out)

            def project_v(g, par):
                for i in range(2):
                    act.wait_ge(full_e[i], 4 * g + 4)
                    copy(vx4[par][:, 2 * i:2 * i + 2, :, 0:HD],
                         ps[6 + i][:, :].rearrange("p (b h d) -> p b h d", b=2, d=HD)).then_inc(empty_e[i], 1)

            def relative(g, par, c):
                bank = rk_bank(c)
                act.wait_ge(full[bank], n_rel(g, bank, c) + 1)
                copy(rk3[:, :, RC * c:RC * (c + 1)],
                     ps[bank][:, :].rearrange("p (l n) -> p n l", n=HB)).then_inc(empty[bank], 1)

            def logits(g, par, u):
                if u % 2:
                    act.wait_ge(centred, H * g + u + 1)
                    part = rq3[:, GB * (u - 1):GB * (u + 1), :]
                    nc.scalar.activation(part, part, ACT.Exp, scale=SCALE).then_inc(exp_done, 1)

            def probT(g, par, u):
                if u % 2 == 0:
                    act.wait_ge(full[4], n_probT(g, u) + 1)
                    copy(rk[:, TOK * u:TOK * (u + 1)], ps[4][:, :]).then_inc(empty[4], 1)

            def weigh(g, par, q):
                act.wait_ge(full[4], n_pv(g, q) + 1)
                if past(g) or q > 1:
                    act.wait_ge(full[5], n_pv(g, q) - 5)
                copy(pv[q % 2][:, :], ps[4][:, :]).then_inc(empty[4], 1)

            def weigh_rel(g, par, c):
                if c % 2 == 0:
                    act.wait_ge(full[0], n_av(g, c) + 1)
                    copy(oav[:, 512 * c:512 * (c + 1)], ps[0][:, :]).then_inc(empty[0], 1)

            def transpose2(g, par):
                for c in range(CT):
                    act.wait_ge(full_m[c], 4 * g + 1)
                    copy(nT[:, c * GB:(c + 1) * GB, 1:S + 1],
                         ps[6 + c][:, :].rearrange("p (b s) -> p b s", b=GB)).then_inc(empty_m[c], 1)

            def keys(g, par):
                for e in range(CT):
                    act.wait_ge(full_m[e], 4 * g + 3)
                    nc.scalar.activation(kact[:, e * TOK:(e + 1) * TOK], ps[6 + e][:, :],
                                         ACT.Relu).then_inc(empty_m[e], 1)

            def gates(g, par):
                act.wait_ge(mixed, 2 * CT * (g + 1))
                for i in range(2):
                    act.wait_ge(full_m[i], 4 * g + 2)
                    nc.scalar.activation(norm[:, TOK * i:TOK * (i + 1)], ps[6 + i][:, :], ACT.Tanh,
                                         scale=0.5).then_inc(empty_m[i], 1)

            pipeline(act, dict(transpose1=transpose1, project_q=project_q, project_k=project_k,
                               project_v=project_v, relative=relative, logits=logits, probT=probT, weigh=weigh,
                               weigh_rel=weigh_rel, transpose2=transpose2, keys=keys, gates=gates))

        @block.vector
        def _(dve):
            vec = nc.vector
            done = [0]

            def link(ins):
                done[0] += 1
                ins.then_inc(setup_v, 1)
                dve.wait_ge(setup_v, done[0])

            def split_table(tab, x, left, rows):
                for n in range(NPART):
                    part = tab[:, n * TW:(n + 1) * TW]
                    link(vec.tensor_copy(part, x))
                    if n < NPART - 1:
                        link(vec.tensor_tensor(left, x, part, ALU.subtract))
                    x = left

            dve.wait_ge(const_in, N_CONST)
            for t in (ekf, eqf):
                link(vec.tensor_copy(t[:, 0:R - 1], t[:, R - 1:R].broadcast_to([HD, R - 1])))
                link(vec.tensor_copy(t[:, 3 * R:TW], t[:, 3 * R - 1:3 * R].broadcast_to([HD, R - 1])))
            link(vec.tensor_copy(ekr, ekf[:, ::-1]))
            link(vec.memset(ones, 1.0))
            link(vec.tensor_tensor(prod, ekf, eqf, ALU.mult))
            split_table(k_tab, ekr, rest, HD)
            split_table(q_tab, eqf, rest, HD)
            dve.wait_ge(pp_sum, 1)
            link(vec.tensor_copy(pp, ps[7][0:1, 0:TW]))
            split_table(pp_tab, pp, rest[0:1, :], 1)
            link(vec.tensor_tensor(pos0[:, :], pos0[:, :], norm[:, 0:D], ALU.add))
            link(vec.tensor_tensor(dtype_[:, :], norm[:, D:2 * D], norm[:, 0:D], ALU.subtract))
            for i in range(2):
                link(vec.memset(ks[i][KR:KR1, :], 1.0))
            assert done[0] == N_SETUP_V
            dve.wait_ge(setup_g, N_SETUP_G)

            def layernorm(kind, g, src, dst):
                for b in range(GB):
                    vec.bn_stats(bn[kind][:, 6 * b:6 * b + 6], src[:, b * D:(b + 1) * D]).then_inc(stats[kind], 1)
                for b in range(GB):
                    dve.wait_ge(stats[kind], GB * g + b + 1)
                    apart(dve)
                    vec.bn_aggr(mv[kind][:, 2 * b:2 * b + 2], bn[kind][:, 6 * b:6 * b + 6]).then_inc(meanvar[kind], 1)
                dve.wait_ge(rstd_ready[kind], g + 1)
                for b in range(GB):
                    vec.tensor_scalar(dst[:, b * D:(b + 1) * D], src[:, b * D:(b + 1) * D],
                                      mv[kind][:, 2 * b:2 * b + 1], rstd[kind][:, b:b + 1],
                                      ALU.subtract, ALU.mult).then_inc(normed[kind], 1)

            def embed(g, par):
                dve.wait_ge(ids_in, 32 * (g + 1))
                vec.tensor_copy(tyf[:, :], tyt[:, :]).then_inc(tyf_ready, 1)
                dve.wait_ge(tyf_ready, g + 1)
                dve.wait_ge(pos_added, g + 1)
                for b in range(GB):
                    row = h[par][:, b * D:(b + 1) * D]
                    vec.scalar_tensor_tensor(row, dtype_[:, :], tyf[:, b:b + 1], row, ALU.mult, ALU.add)\
                       .then_inc(x_ready, 1)
                dve.wait_ge(x_ready, GB * (g + 1))
                layernorm(0, g, h[par], h[par])

            def norm1(g, par):
                dve.wait_ge(h_ready, g + 1)
                if past(g, 2):
                    dve.wait_ge(result, 2 * (g - 1))
                layernorm(1, g, h[par], norm)

            def split(g, n, parts):
                for e in range(CT):
                    dve.wait_ge(part0, 4 * g + 2 * n + e + 1)
                    if past(g) or n > 0:
                        dve.wait_ge(part2, 4 * g + 2 * n)
                    vec.tensor_tensor(norm[:, e * TOK:(e + 1) * TOK], ps[6 + e][:, :],
                                      parts[:, 0, e * TOK:(e + 1) * TOK], ALU.subtract)\
                       .then_inc(empty_e[e], 1)
                for e in range(CT):
                    dve.wait_ge(part1, 4 * g + 2 * n + e + 1)
                    vec.tensor_tensor(parts[:, 2, e * TOK:(e + 1) * TOK], norm[:, e * TOK:(e + 1) * TOK],
                                      parts[:, 1, e * TOK:(e + 1) * TOK], ALU.subtract).then_inc(part2, 1)

            def project_q(g, par):
                if past(g):
                    dve.wait_ge(q_out, 16 * NPART * g)
                split(g, 0, qp)

            def project_k(g, par):
                if past(g):
                    dve.wait_ge(k_out, 16 * NPART * g)
                split(g, 1, kp)

            def relative(g, par, c):
                bank = rq_bank(c)
                if c == 0:
                    if past(g):
                        dve.wait_ge(oav_out, 64 * g)
                dve.wait_ge(full[bank], n_rel(g, bank, c) + 1)
                vec.tensor_copy(rq3[:, :, RC * c:RC * (c + 1)],
                                ps[bank][:, :].rearrange("p (m n) -> p n m", n=HB)).then_inc(empty[bank], 1)

            def logits(g, par, u):
                bank = 2 + u % 2
                if u == 0:
                    for n in (1, 3):
                        dve.wait_ge(empty[n], n_rel(g, n, NRC))
                dve.wait_ge(full[bank], n_logit(g, u) + 1)
                apart(dve)
                for b in range(GB):
                    n = GB * u + b
                    ins = vec.tensor_tensor_reduce(out=rq3[:, n, :], in0=ps[bank][:, b * S:(b + 1) * S],
                                                   in1=rq3[:, n, :], scale=1.0, scalar=LOWEST, op0=ALU.add,
                                                   op1=ALU.max, accum_out=mx[:, n:n + 1])
                ins.then_inc(empty[bank], 1)

            def probT(g, par, u):
                if u % 2:
                    dve.wait_ge(full[5], n_probT(g, u) + 1)
                    vec.tensor_copy(rk[:, TOK * u:TOK * (u + 1)], ps[5][:, :]).then_inc(empty[5], 1)

            def turn(g, par, q):
                dve.wait_ge(full[5], n_pv(g, q) + 1)
                if q == 0:
                    if past(g):
                        dve.wait_ge(o_sum, g)
                vec.tensor_copy(ot4[:, :, 4 * q:4 * q + 4, :],
                                ps[5][:, :].rearrange("p (b j c) -> p b j c", b=GB, j=4)[:, :, :, 0:VW])\
                   .then_inc(empty[5], 1)

            def weigh_rel(g, par, c):
                if c % 2:
                    dve.wait_ge(full[1], n_av(g, c) + 1)
                    vec.tensor_copy(oav[:, 512 * c:512 * (c + 1)], ps[1][:, :]).then_inc(empty[1], 1)

            def combine(g, par):
                dve.wait_ge(empty[5], USES[5] * (g + 1))
                vec.reciprocal(rden[:, :], ot3[:, :, HD]).then_inc(rden_ready, 1)
                dve.wait_ge(part2, 4 * embeds_before_mix(g))
                dve.wait_ge(orel_in, 16 * (g + 1))
                vec.tensor_tensor(norm[:, :].rearrange("p (b h d) -> p b h d", b=GB, d=HD), ot4[:, :, :, 0:HD],
                                  orel[:, :].rearrange("p (d h b) -> p b h d", d=HD, b=GB), ALU.add)\
                   .then_inc(o_sum, 1)
                dve.wait_ge(o_sum, g + 1)
                dve.wait_ge(rden_ready, g + 1)
                n3 = norm[:, :].rearrange("p (n d) -> p n d", d=HD)
                vec.tensor_tensor(n3, n3, rden[:, :].unsqueeze(2).broadcast_to([P, HB, HD]), ALU.mult)\
                   .then_inc(o_norm, 1)

            def norm2(g, par):
                dve.wait_ge(h2_ready, g + 1)
                layernorm(2, g, h[par], norm)

            def shift(g, par):
                for c in range(CT):
                    dve.wait_ge(empty_m[c], 4 * g + 1)
                vec.tensor_tensor(norm[:, :].rearrange("p (n s) -> p n s", s=S), nT[:, :, 1:S + 1], nT[:, :, 0:S],
                                  ALU.subtract).then_inc(diff_ready, 1)
                dve.wait_ge(diff_ready, g + 1)
                for dst, mu in ((xr, mur), (xk, muk)):
                    for c in range(CT):
                        vec.scalar_tensor_tensor(
                            dst[:, c * TOK:(c + 1) * TOK].rearrange("p (b s) -> p b s", b=GB),
                            norm[:, c * TOK:(c + 1) * TOK].rearrange("p (b s) -> p b s", b=GB), mu[:, c:c + 1],
                            nT[:, c * GB:(c + 1) * GB, 0:S], ALU.mult, ALU.add).then_inc(mixed, 1)

            def values(g, par):
                for i in range(2):
                    half = slice(TOK * i, TOK * (i + 1))
                    dve.wait_ge(empty_m[i], 4 * g + 2)
                    dve.wait_ge(full_m[i], 4 * g + 4)
                    vec.scalar_tensor_tensor(norm[:, half], norm[:, half], 1.0, ps[6 + i][:, :], ALU.add, ALU.mult)\
                       .then_inc(empty_m[i], 1)
                    dve.wait_ge(empty_m[i], 4 * g + 4)
                    vec.scalar_tensor_tensor(h[par][:, half], norm[:, half], 0.5, h[par][:, half], ALU.mult, ALU.add)\
                       .then_inc(result, 1)

            pipeline(dve, dict(embed=embed, norm1=norm1, project_q=project_q, project_k=project_k,
                               relative=relative, logits=logits, probT=probT, turn=turn, weigh_rel=weigh_rel,
                               combine=combine, norm2=norm2, shift=shift, values=values))

        @block.tensor
        def _(pe):
            mm = nc.tensor.matmul
            pe.wait_ge(const_in, N_CONST)
            pe.wait_ge(setup_v, 4 + 3)
            mm(ps[7][0:1, 0:TW], ones, prod, start=True, stop=True).then_inc(pp_sum, 1)
            pe.wait_ge(setup_g, N_SETUP_G)
            pe.wait_ge(slots_in, 16 * (2 * SLOTS + NPART))

            def transpose(dst, src, **kw):
                return mm(dst, src, ident[:, :], is_transpose=True, **kw)

            def transpose1(g, par):
                pe.wait_ge(normed[1], GB * (g + 1))
                for c in range(CT):
                    if past(g):
                        pe.wait_ge(empty_e[c], 4 * g)
                    if past(g, 2):
                        pe.wait_ge(empty_m[c], 4 * (g - 1))
                    for b in range(GB):
                        ins = transpose(ps[6 + c][:, b * S:(b + 1) * S], norm[:, b * D + c * P:b * D + (c + 1) * P],
                                        start=True, stop=True)
                    ins.then_inc(full_e[c], 1)

            def project(g, w, use, full_, empty_, src):
                for e in range(CT):
                    pe.wait_ge(empty_[e], 4 * g + use)
                    for c in range(CT):
                        ins = mm(ps[6 + e][:, :], w[:, c * D + e * P:c * D + (e + 1) * P], src(c),
                                 start=c == 0, stop=c == CT - 1)
                    ins.then_inc(full_[e], 1)

            def project_rows(g, w, use, full_, empty_, src):
                for i in range(2):
                    pe.wait_ge(empty_[i], 4 * g + use)
                    for n in range(2):
                        for c in range(CT):
                            ins = mm(ps[6 + i][:, n * D:(n + 1) * D], src(c, 2 * i + n), w[:, c * D:(c + 1) * D],
                                     start=c == 0, stop=c == CT - 1)
                    ins.then_inc(full_[i], 1)

            def normT_tile(c):
                return nT[:, c * GB:(c + 1) * GB, 1:S + 1]

            def project_q(g, par):
                for c in range(CT):
                    pe.wait_ge(empty_e[c], 4 * g + 1)
                project(g, w_q, 1, full_e, empty_e, normT_tile)

            def project_k(g, par):
                project(g, w_k, 2, full_e, empty_e, normT_tile)

            def project_v(g, par):
                project_rows(g, w_v, 3, full_e, empty_e, lambda c, b: nT[:, c * GB + b, 1:S + 1])

            def relative(g, par, c):
                if c == 0:
                    pe.wait_ge(q_in, 16 * SLOTS * (g + 1))
                    pe.wait_ge(k_in, 16 * SLOTS * (g + 1))
                bank = rk_bank(c)
                if past(g) or c > 1:
                    pe.wait_ge(empty[bank], n_rel(g, bank, c))
                for i in range(RC):
                    l = RC * c + i
                    ins = mm(ps[bank][:, i * HB:(i + 1) * HB], ekw[0:KR, S - 1 - l:TW - l], qs3[par][0:KR, :, l],
                             start=True, stop=True)
                ins.then_inc(full[bank], 1)
                bank = rq_bank(c)
                if past(g) or c > 1:
                    pe.wait_ge(empty[bank], n_rel(g, bank, c))
                for i in range(RC):
                    m = RC * c + i
                    ins = mm(ps[bank][:, i * HB:(i + 1) * HB], eqw[0:KR1, S - 1 - m:TW - m], ks3[par][0:KR1, :, m],
                             start=True, stop=True)
                ins.then_inc(full[bank], 1)

            def logits(g, par, u):
                bank = 2 + u % 2
                if u == 0:
                    for n in (0, 2):
                        pe.wait_ge(empty[n], n_rel(g, n, NRC))
                pe.wait_ge(empty[bank], n_logit(g, u))
                for b in range(GB):
                    n = GB * u + b
                    dst = ps[bank][:, b * S:(b + 1) * S]
                    mm(dst, qs3[par][0:KR, n, :], ks3[par][0:KR, n, :], start=True, stop=False)
                    ins = transpose(dst, rk3[:, n, :], start=False, stop=True)
                ins.then_inc(full[bank], 1)

            def probT(g, par, u):
                bank = 4 + u % 2
                pe.wait_ge(exp_done, H // 2 * g + u // 2 + 1)
                if past(g) or u > 1:
                    pe.wait_ge(empty[bank], n_probT(g, u))
                for b in range(GB):
                    ins = transpose(ps[bank][:, b * S:(b + 1) * S], rq3[:, GB * u + b, :], start=True, stop=True)
                ins.then_inc(full[bank], 1)

            def weigh(g, par, q):
                for n in (4, 5):
                    pe.wait_ge(empty[n], n_pv(g, q))
                for i in range(2):
                    if q == 0:
                        pe.wait_ge(empty_e[i], 4 * (g + 1))
                for b in range(GB):
                    for j in range(4):
                        hd = 4 * q + j
                        ins = mm(ps[4][32 * j:32 * j + VW, b * S:(b + 1) * S], vx4[par][:, b, hd, :],
                                 rk3[:, GB * hd + b, :], start=True, stop=True, tile_position=(0, 32 * j))
                ins.then_inc(full[4], 1)

            def turn(g, par, q):
                pe.wait_ge(empty[4], n_pv(g, q) + 1)
                pe.wait_ge(empty[5], n_pv(g, q))
                for b in range(GB):
                    ins = transpose(ps[5][:, b * P:(b + 1) * P], pv[q % 2][:, b * S:(b + 1) * S], start=True, stop=True)
                ins.then_inc(full[5], 1)

            def weigh_rel(g, par, c):
                bank = c % 2
                pe.wait_ge(empty[bank], n_av(g, c))
                for i in range(8):
                    for j in range(4):
                        l = 32 * j + 8 * c + i
                        ins = mm(ps[bank][32 * j:32 * j + HD, i * HB:(i + 1) * HB], avt[:, (S - 1 - l) * HD:(S - l) * HD],
                                 rk3[:, :, l], start=True, stop=True, tile_position=(0, 32 * j))
                ins.then_inc(full[bank], 1)

            def transpose2(g, par):
                pe.wait_ge(normed[2], GB * (g + 1))
                for c in range(CT):
                    if isinstance(g, int):
                        pe.wait_ge(empty_m[c], 4 * g)
                    pe.wait_ge(empty_e[c], 4 * embeds_before_mix(g))
                    for b in range(GB):
                        ins = transpose(ps[6 + c][:, b * S:(b + 1) * S], norm[:, b * D + c * P:b * D + (c + 1) * P],
                                        start=True, stop=True)
                    ins.then_inc(full_m[c], 1)

            def keys(g, par):
                pe.wait_ge(mixed, 2 * CT * (g + 1))
                project(g, w_fk, 2, full_m, empty_m, lambda c: xk[:, c * TOK:(c + 1) * TOK])

            def gates(g, par):
                pe.wait_ge(mixed, 2 * CT * g + CT)
                project_rows(g, w_r, 1, full_m, empty_m,
                             lambda c, b: xr[:, c * TOK + b * S:c * TOK + (b + 1) * S])

            def values(g, par):
                pe.wait_ge(squared, CT * (g + 1))
                project_rows(g, w_fv, 3, full_m, empty_m,
                             lambda c, b: kact[:, c * TOK + b * S:c * TOK + (b + 1) * S])

            pipeline(pe, dict(transpose1=transpose1, project_q=project_q, project_k=project_k, project_v=project_v,
                              relative=relative, logits=logits, probT=probT, weigh=weigh, turn=turn,
                              weigh_rel=weigh_rel, transpose2=transpose2, keys=keys, gates=gates, values=values))


_INS = ['ids', 'types', 'word', 'pos', 'typ', 'gamma', 'beta', 'wq', 'wk', 'wv', 'eq', 'ek', 'ev',
        'wr_t', 'wk_t', 'wv_t', 'mu_r', 'mu_k']


def kernel(**inputs):
    import numpy as np
    import concourse.bacc as bacc
    from concourse.bass_utils import run_bass_kernel_spmd

    x = {k: np.asarray(v) for k, v in inputs.items()}

    def by_group(a):
        return a.reshape(NG, GB, S).transpose(0, 2, 1)

    data = dict(
        ids=by_group(x['x']), types=by_group(x['mask_BS_i1_0']), word=x['L0_tok_word_emb'],
        pos=x['L0_tok_pos_emb'], typ=x['L0_tok_type_emb'], gamma=x['L0_tok_gamma'], beta=x['L0_tok_beta'],
        wq=x['L0_attn_Wq'], wk=x['L0_attn_Wk'], wv=x['L0_attn_Wv'], eq=x['L0_attn_Eq'].T, ek=x['L0_attn_Ek'].T,
        ev=x['L0_attn_Ev'][::-1], wr_t=x['L0_ffn_W_r'].T, wk_t=x['L0_ffn_W_k'].T, wv_t=x['L0_ffn_W_v'].T,
        mu_r=x['L0_ffn_mu_r'].reshape(CT, P).T, mu_k=x['L0_ffn_mu_k'].reshape(CT, P).T)
    nc = bacc.Bacc("TRN2", target_bir_lowering=False, num_devices=1, dynamic_dma_scratch_size=8192)
    arrays, args = {}, []
    for name in _INS:
        a = np.ascontiguousarray(data[name])
        arrays[f"in_{name}"] = a
        args.append(nc.dram_tensor(f"in_{name}", a.shape, mybir.dt.from_np(a.dtype), kind="ExternalInput").ap())
    out = nc.dram_tensor("out", (B, S, D), fp32, kind="ExternalOutput").ap()
    tower_kernel(nc, *args, out.rearrange("(g b) s n -> g s b n", b=GB))
    r = run_bass_kernel_spmd(nc, [arrays], core_ids=[0])
    return r.results[0]["out"]
```

```python
import concourse.bass as bass
from concourse import mybir
from contextlib import ExitStack

fp32 = mybir.dt.float32
bf16 = mybir.dt.bfloat16
i32 = mybir.dt.int32
ALU = mybir.AluOpType
ACT = mybir.ActivationFunctionType

P = 128
B, S, D = 128, 128, 256
H, HD = 16, 16
R = 64
GB = 4
NG = B // GB
TOK = GB * S
HB = H * GB
CT = D // P
NPART = 3
SLOTS = 6
TW = 2 * S - 1
VW = HD + 1
Q_PART = (0, 0, 0, 1, 1, 2)
K_PART = (0, 1, 2, 0, 1, 0)
KR = SLOTS * HD
KR1 = KR + NPART
RC = 8
NRC = S // RC
LAG = 4
SCALE = 1.0 / HD ** 0.5
LOWEST = -3.4028234e38
EPS_EMBED, EPS_NORM = 1e-12, 1e-5


def tower_kernel(nc, ids, types, word, pos, typ, gamma, beta, wq, wk, wv, eq, ek, ev,
                 wr_t, wk_t, wv_t, mu_r, mu_k, out):
    ctx = ExitStack()
    with ctx:
        def sb(name, shape, dt=fp32):
            return ctx.enter_context(nc.sbuf_tensor(name, shape, dt))

        def sem(name):
            return ctx.enter_context(nc.semaphore(name))

        rk = sb("rk", [P, HB * S])
        rq = sb("rq", [P, HB * S])
        qs = [sb(f"qs{i}", [P, HB * S], bf16) for i in range(2)]
        ks = [sb(f"ks{i}", [P, HB * S], bf16) for i in range(2)]
        vx = [sb(f"vx{i}", [P, GB * H * VW]) for i in range(2)]
        h = [sb(f"h{i}", [P, GB * D]) for i in range(2)]
        h2 = sb("h2", [P, GB * D])
        rows = sb("rows", [P, GB * D])
        mrows = sb("mrows", [P, GB * D])
        normT = sb("normT", [P, CT * GB * (S + 1)])
        parts = sb("parts", [P, NPART * CT * TOK], bf16)
        pv = sb("pv", [P, TOK])
        ot = sb("ot", [P, HB * VW])
        orel = sb("orel", [P, HD * HB])
        xrk = sb("xrk", [P, 2 * CT * TOK])
        xr, xk = xrk[:, 0:CT * TOK], xrk[:, CT * TOK:]
        kact = xr
        oav = xrk
        avt = sb("avt", [P, S * HD])
        ekw = sb("ekw", [P, TW], bf16)
        eqw = sb("eqw", [P, TW], bf16)
        w_q, w_k, w_v, w_r, w_fk, w_fv = (sb(n, [P, CT * D]) for n in
                                          ("w_q", "w_k", "w_v", "w_r", "w_fk", "w_fv"))
        ident = sb("ident", [P, P])
        pos0 = sb("pos0", [P, D])
        dtype_ = sb("dtype_", [P, D])
        gam = sb("gam", [P, D])
        bet = sb("bet", [P, D])
        mur = sb("mur", [P, CT])
        muk = sb("muk", [P, CT])
        neghalf = sb("neghalf", [P, GB])
        idt = sb("idt", [P, GB], i32)
        tyt = sb("tyt", [P, GB], i32)
        tyf = sb("tyf", [P, GB])
        bn = [sb(f"bn{i}", [P, GB * 6]) for i in range(3)]
        mv = [sb(f"mv{i}", [P, GB * 2]) for i in range(3)]
        rstd = [sb(f"rstd{i}", [P, GB]) for i in range(3)]
        mx = sb("mx", [P, HB])
        rden = sb("rden", [P, HB])
        ekf = rk[0:HD, 0:TW]
        ekr = rk[0:HD, TW:2 * TW]
        eqf = rk[0:HD, 2 * TW:3 * TW]
        prod = rk[0:HD, 3 * TW:4 * TW]
        rest = rk[0:HD, 4 * TW:5 * TW]
        ones = rk[0:HD, 5 * TW:5 * TW + 1]
        pp = rk[0:1, 6 * TW:7 * TW]
        k_tab = qs[0][0:HD, 0:NPART * TW]
        q_tab = qs[1][0:HD, 0:NPART * TW]
        pp_tab = ks[0][0:1, 0:NPART * TW]

        ps = [ctx.enter_context(nc.psum_tensor(f"ps{i}", [P, 512], fp32)) for i in range(8)]

        ev_wide = nc.dram_tensor("ev_wide", [TW, HD], fp32, kind="Internal")
        q_dram = nc.dram_tensor("q_dram", [NPART, D, TOK], bf16, kind="Internal").ap()
        k_dram = nc.dram_tensor("k_dram", [NPART, D, TOK], bf16, kind="Internal").ap()
        o_dram = nc.dram_tensor("o_dram", [HD, S, HB], fp32, kind="Internal").ap()

        rk3 = rk[:, :].rearrange("p (n l) -> p n l", l=S)
        rq3 = rq[:, :].rearrange("p (n m) -> p n m", m=S)
        qs3 = [t[:, :].rearrange("p (n l) -> p n l", l=S) for t in qs]
        ks3 = [t[:, :].rearrange("p (n l) -> p n l", l=S) for t in ks]
        vx4 = [t[:, :].rearrange("p (b h c) -> p b h c", b=GB, c=VW) for t in vx]
        nT = normT[:, :].rearrange("p (n s) -> p n s", s=S + 1)
        parts3 = parts[:, :].rearrange("p (k t) -> p k t", k=NPART)
        ot3 = ot[:, :].rearrange("p (n c) -> p n c", c=VW)
        ot4 = ot[:, :].rearrange("p (b h c) -> p b h c", b=GB, c=VW)

        const_in = sem("const_in")
        setup_v = sem("setup_v")
        setup_g = sem("setup_g")
        pp_sum = sem("pp_sum")
        slots_in = sem("slots_in")
        wide_out = sem("wide_out")
        full = [sem(f"full{i}") for i in range(6)]
        empty = [sem(f"empty{i}") for i in range(6)]
        full_e = sem("full_e")
        empty_e = sem("empty_e")
        full_m = sem("full_m")
        empty_m = sem("empty_m")
        ids_in = sem("ids_in")
        words_in = sem("words_in")
        pos_added = sem("pos_added")
        tyf_ready = sem("tyf_ready")
        x_ready = sem("x_ready")
        stats = [sem(f"stats{i}") for i in range(3)]
        meanvar = [sem(f"meanvar{i}") for i in range(3)]
        eps_added = [sem(f"eps_added{i}") for i in range(3)]
        rstd_ready = [sem(f"rstd_ready{i}") for i in range(3)]
        normed = [sem(f"normed{i}") for i in range(3)]
        scaled = sem("scaled")
        h_ready = sem("h_ready")
        part0 = sem("part0")
        part1 = sem("part1")
        part2 = sem("part2")
        q_out = [sem(f"q_out{e}") for e in range(CT)]
        k_out = [sem(f"k_out{e}") for e in range(CT)]
        q_in = sem("q_in")
        k_in = sem("k_in")
        centred = sem("centred")
        exp_done = sem("exp_done")
        oav_out = sem("oav_out")
        orel_in = sem("orel_in")
        rden_ready = sem("rden_ready")
        o_sum = sem("o_sum")
        h2_ready = sem("h2_ready")
        o_norm = sem("o_norm")
        diff_ready = sem("diff_ready")
        mixed = sem("mixed")
        squared = sem("squared")
        gated = sem("gated")
        result = sem("result")
        stored = sem("stored")
        passed = sem("passed")

        N_CONST = 16 * (6 + 5 + 2 + 2 + 1)
        N_SETUP_G = 4 + 2
        N_SETUP_V = 4 + 3 + 3 * 5 + 1 + 2 + 2
        EPS = (EPS_EMBED, EPS_NORM, EPS_NORM)

        USES = (14, 14, 16, 16, 8, 8)
        EMBED_USES = ("t0", "t1", "q0", "q1", "v0", "k0", "v1", "k1")
        MIX_USES = ("t0", "t1", "r0", "r1", "k0", "k1", "v0", "v1")

        def n_rel(g, bank, c):
            return g * USES[bank] + c // 2

        def n_logit(g, u):
            return g * USES[2] + NRC // 2 + u // 2

        def n_probT(g, u):
            return g * USES[4] + u // 2

        def n_pv(g, q):
            return g * USES[0] + NRC // 2 + q

        def n_av(g, c):
            return g * USES[0] + NRC // 2 + H // 4 + c // 2

        def n_embed(g, use):
            return g * len(EMBED_USES) + EMBED_USES.index(use)

        def n_mix(g, use):
            return g * len(MIX_USES) + MIX_USES.index(use)

        def rk_bank(c):
            return (0, 2)[c % 2]

        def rq_bank(c):
            return (1, 3)[c % 2]

        def past(g, n=1):
            return not isinstance(g, int) or g >= n

        def apart(eng):
            eng.sem_inc(passed, 1)

        MIX_AT = ((8, "combine"), (9, "residual"), (11, "stats2"), (12, "root2"), (13, "apply2"),
                  (14, "turn2", 0), (15, "turn2", 1), (17, "diff"), (18, "mix_r"), (19, "mix_k"),
                  (20, "gate", 0), (21, "gate", 1), (22, "key", 0), (23, "key", 1), (23, "square", 0),
                  (24, "square", 1), (25, "value", 0), (26, "value", 1), (27, "store"))
        EMBED_AT = ((0, "fetch"), (10, "gather", 0), (11, "gather", 1), (12, "gather", 2), (13, "gather", 3),
                    (16, "position"), (17, "type"), (18, "root0"), (19, "apply0"), (20, "gamma"), (21, "beta"),
                    (22, "stats1"), (23, "root1"), (24, "apply1"), (25, "turn1", 0), (26, "turn1", 1),
                    (27, "q", 0), (28, "q", 1), (28, "q_parts", 0), (29, "v", 0), (29, "q_parts", 1), (30, "k", 0),
                    (31, "v", 1), (31, "k_parts", 0), (32, "k", 1), (33, "k_parts", 1))

        def order(attend, mix, embed):
            steps = []
            for slot in range(NRC + H + LAG + 4):
                steps += [tuple(x) for at, *x in (MIX_AT if mix else ()) if at == slot]
                steps += [tuple(x) for at, *x in (EMBED_AT if embed else ()) if at == slot]
                if not attend:
                    continue
                u, c = slot - NRC, slot - NRC - H - LAG
                if u < 0:
                    steps.append(("relative", slot))
                elif c < 0:
                    if u < H:
                        steps.append(("logits", u))
                    v = u - LAG
                    if v > 0 and v % 4 == 0:
                        steps.append(("weigh", v // 4 - 1))
                    if v > 1 and v % 4 == 1:
                        steps.append(("turn", v // 4 - 1))
                    if v >= 0:
                        steps.append(("probT", v))
                else:
                    if c == 0:
                        steps.append(("weigh", H // 4 - 1))
                    if c == 1:
                        steps.append(("turn", H // 4 - 1))
                    steps.append(("weigh_rel", c))
            if attend:
                steps.append(("store_rel",))
            return steps

        MIX = {x[1] for x in MIX_AT}
        EMBED = {x[1] for x in EMBED_AT}

        def run(steps, table, g, par):
            for name, *arg in steps:
                if name in table:
                    d = -1 if name in MIX else 1 if name in EMBED else 0
                    table[name](g + d, (par + d) % 2, *arg)

        def pipeline(eng, table):
            run(order(False, False, True), table, -1, 1)
            run(order(True, False, True), table, 0, 0)
            with eng.Fori(0, NG // 2 - 1) as t:
                for i in (1, 2):
                    run(order(True, True, True), table, t * 2 + i, i % 2)
            run(order(True, True, False), table, NG - 1, 1)
            run(order(False, True, False), table, NG, 0)

        block = ctx.enter_context(nc.Block())

        @block.sync
        def _(sp):
            def load(dst, src):
                sp.dma_start(dst, src).then_inc(const_in, 16)

            for dst, src in ((w_q, wq), (w_k, wk), (w_v, wv), (w_r, wr_t), (w_fk, wk_t), (w_fv, wv_t)):
                load(dst[:, :].rearrange("p (c n) -> p c n", c=CT), src.rearrange("(c p) n -> p c n", p=P))
            load(pos0[:, :], pos)
            load(gam[:, :], bass.AP(gamma.tensor, 0, [[0, P], [1, D]]))
            load(bet[:, :], bass.AP(beta.tensor, 0, [[0, P], [1, D]]))
            load(mur[:, :], mu_r)
            load(muk[:, :], mu_k)
            load(rows[:, 0:D], bass.AP(typ.tensor, 0, [[0, P], [1, D]]))
            load(rows[:, D:2 * D], bass.AP(typ.tensor, D, [[0, P], [1, D]]))
            load(ekf[:, R - 1:3 * R], ek)
            load(eqf[:, R - 1:3 * R], eq)
            wide = ev_wide.ap()
            sp.dma_start(wide[0:R - 1, :], bass.AP(ev.tensor, 0, [[0, R - 1], [1, HD]])).then_inc(wide_out, 16)
            sp.dma_start(wide[R - 1:3 * R, :], ev).then_inc(wide_out, 16)
            sp.dma_start(wide[3 * R:TW, :], bass.AP(ev.tensor, 2 * R * HD, [[0, R - 1], [1, HD]])).then_inc(wide_out, 16)
            sp.wait_ge(wide_out, 48)
            load(avt[:, :], bass.AP(ev_wide, 0, [[HD, P], [1, S * HD]]))
            sp.wait_ge(setup_v, N_SETUP_V)
            for s in range(SLOTS):
                sp.dma_start(ekw[s * HD:(s + 1) * HD, :], k_tab[:, K_PART[s] * TW:(K_PART[s] + 1) * TW]).then_inc(slots_in, 16)
                sp.dma_start(eqw[s * HD:(s + 1) * HD, :], q_tab[:, Q_PART[s] * TW:(Q_PART[s] + 1) * TW]).then_inc(slots_in, 16)
            for s in range(NPART):
                sp.dma_start(eqw[KR + s:KR + s + 1, :], pp_tab[:, s * TW:(s + 1) * TW]).then_inc(slots_in, 16)
            sp.wait_ge(slots_in, 16 * (2 * SLOTS + NPART))

            def fetch(g, par):
                if past(g):
                    sp.wait_ge(words_in, 16 * GB * g)
                if past(g):
                    sp.wait_ge(tyf_ready, g)
                    apart(sp)
                sp.dma_start(idt[:, :], ids[g]).then_inc(ids_in, 16)
                sp.dma_start(tyt[:, :], types[g]).then_inc(ids_in, 16)

            def parts_to_dram(g, e, dram, n_parts, out_done, in_done):
                if e == 0 and past(g):
                    sp.wait_ge(in_done, 16 * SLOTS * g)
                    apart(sp)
                sp.wait_ge(part2, n_parts)
                sp.dma_start(dram.rearrange("k (c p) t -> c p k t", p=P)[e],
                             parts3[:, :, e * TOK:(e + 1) * TOK]).then_inc(out_done[e], 16)

            def parts_to_slots(g, dram, slots, part_of, out_done, in_done):
                for e in range(CT):
                    sp.wait_ge(out_done[e], 16 * (g + 1))
                for s in range(SLOTS):
                    sp.dma_start(slots[s * HD:(s + 1) * HD, :].rearrange("p (n t) -> p n t", t=TOK),
                                 dram[part_of[s]].rearrange("(n d) t -> d n t", d=HD)).then_inc(in_done, 16)

            def q_parts(g, par, e):
                parts_to_dram(g, e, q_dram, 4 * g + e + 1, q_out, q_in)
                if e == 1:
                    parts_to_slots(g, q_dram, qs[par], Q_PART, q_out, q_in)

            def k_parts(g, par, e):
                parts_to_dram(g, e, k_dram, 4 * g + 2 + e + 1, k_out, k_in)
                if e == 1:
                    parts_to_slots(g, k_dram, ks[par], K_PART, k_out, k_in)

            def store_rel(g, par):
                if past(g):
                    sp.wait_ge(orel_in, 16 * g)
                    apart(sp)
                    sp.wait_ge(stored, 16 * g)
                    apart(sp)
                for n in range(2):
                    sp.wait_ge(empty[n], (g + 1) * USES[n])
                    apart(sp)
                for j in range(4):
                    sp.dma_start(o_dram[:, 32 * j:32 * j + 32, :].rearrange("d l n -> d (l n)"),
                                 oav[32 * j:32 * j + HD, :]).then_inc(oav_out, 16)
                sp.wait_ge(oav_out, 64 * (g + 1))
                if past(g):
                    sp.wait_ge(o_sum, g)
                    apart(sp)
                sp.dma_start(orel[:, :].rearrange("p (d n) -> p d n", n=HB),
                             o_dram.rearrange("d l n -> l d n")).then_inc(orel_in, 16)

            def store(g, par):
                sp.wait_ge(result, 2 * (g + 1))
                apart(sp)
                sp.dma_start(out[g], h2[:, :].rearrange("p (b n) -> p b n", b=GB)).then_inc(stored, 16)

            pipeline(sp, dict(fetch=fetch, q_parts=q_parts, k_parts=k_parts, store_rel=store_rel, store=store))
            sp.wait_ge(stored, 16 * NG)

        @block.gpsimd
        def _(pool):
            gps = nc.gpsimd
            gps.memset(ident[:, :], 0.0).then_inc(setup_g, 1)
            pool.wait_ge(setup_g, 1)
            gps.affine_select(out=ident[:, :], in_=ident[:, :], compare_op=ALU.not_equal, fill=1.0, base=0,
                              pattern=[[-1, P]], channel_multiplier=1).then_inc(setup_g, 1)
            gps.memset(neghalf[:, :], -0.5).then_inc(setup_g, 1)
            gps.memset(normT[:, :], 0.0).then_inc(setup_g, 1)
            for i in range(2):
                gps.memset(vx[i][:, :], 1.0).then_inc(setup_g, 1)
            pool.wait_ge(setup_g, N_SETUP_G)
            pool.wait_ge(const_in, N_CONST)
            pool.wait_ge(setup_v, N_SETUP_V)

            def inverse_root(kind, g):
                pool.wait_ge(meanvar[kind], GB * (g + 1))
                apart(pool)
                gps.tensor_scalar(rstd[kind][:, :], mv[kind][:, 1::2], EPS[kind], None, ALU.add).then_inc(eps_added[kind], 1)
                pool.wait_ge(eps_added[kind], g + 1)
                gps.tensor_tensor(rstd[kind][:, :], rstd[kind][:, :], neghalf[:, :], ALU.pow).then_inc(rstd_ready[kind], 1)

            def gather(g, par, b):
                if b == 0:
                    pool.wait_ge(ids_in, 32 * (g + 1))
                    if past(g, 2):
                        pool.wait_ge(h2_ready, g - 1)
                        apart(pool)
                gps.indirect_dma_start(h[par][:, b * D:(b + 1) * D], None, word,
                                       bass.IndirectOffsetOnAxis(ap=idt[:, b:b + 1], axis=0)).then_inc(words_in, 16)

            def position(g, par):
                pool.wait_ge(words_in, 16 * GB * (g + 1))
                h3 = h[par][:, :].rearrange("p (b n) -> p b n", b=GB)
                gps.tensor_tensor(h3, h3, pos0[:, :].unsqueeze(1).broadcast_to([P, GB, D]), ALU.add).then_inc(pos_added, 1)

            def gamma_(g, par):
                pool.wait_ge(normed[0], GB * (g + 1))
                h3 = h[par][:, :].rearrange("p (b n) -> p b n", b=GB)
                gps.tensor_tensor(h3, h3, gam[:, :].unsqueeze(1).broadcast_to([P, GB, D]), ALU.mult).then_inc(scaled, 1)

            def beta_(g, par):
                pool.wait_ge(scaled, g + 1)
                h3 = h[par][:, :].rearrange("p (b n) -> p b n", b=GB)
                gps.tensor_tensor(h3, h3, bet[:, :].unsqueeze(1).broadcast_to([P, GB, D]), ALU.add).then_inc(h_ready, 1)

            def logits(g, par, u):
                pool.wait_ge(empty[2 + u % 2], n_logit(g, u) + 1)
                part = rq3[:, GB * u:GB * (u + 1), :]
                gps.tensor_tensor(part, part, mx[:, GB * u:GB * (u + 1)].unsqueeze(2).broadcast_to([P, GB, S]),
                                  ALU.subtract).then_inc(centred, 1)

            def residual(g, par):
                pool.wait_ge(o_norm, g + 1)
                gps.tensor_tensor(h2[:, :], h2[:, :], h[par][:, :], ALU.add).then_inc(h2_ready, 1)

            def square(g, par, e):
                pool.wait_ge(empty_m, n_mix(g, f"k{e}") + 1)
                t = kact[:, e * TOK:(e + 1) * TOK]
                gps.tensor_tensor(t, t, t, ALU.mult).then_inc(squared, 1)

            pipeline(pool, dict(gather=gather, position=position, root0=lambda g, par: inverse_root(0, g),
                                gamma=gamma_, beta=beta_, root1=lambda g, par: inverse_root(1, g), logits=logits,
                                residual=residual, root2=lambda g, par: inverse_root(2, g), square=square))

        @block.scalar
        def _(act):
            act.wait_ge(setup_g, N_SETUP_G)

            def copy(dst, src):
                return nc.scalar.activation(dst, src, ACT.Copy)

            def turned(c):
                return nT[:, c * GB:(c + 1) * GB, 1:S + 1]

            def turn1(g, par, c):
                act.wait_ge(full_e, n_embed(g, f"t{c}") + 1)
                if past(g, 2):
                    act.wait_ge(mixed, 2 * CT * (g - 1))
                copy(turned(c), ps[6][:, :].rearrange("p (b s) -> p b s", b=GB)).then_inc(empty_e, 1)

            def first_part(g, e, use, out_done, n_out):
                act.wait_ge(full_e, n_embed(g, use) + 1)
                if not isinstance(n_out, int) or n_out > 0:
                    act.wait_ge(out_done[e], n_out)
                copy(parts3[:, 0, e * TOK:(e + 1) * TOK], ps[6][:, :]).then_inc(part0, 1)

            def second_part(g, e, use):
                act.wait_ge(empty_e, n_embed(g, use) + 1)
                copy(parts3[:, 1, e * TOK:(e + 1) * TOK], rows[:, e * TOK:(e + 1) * TOK]).then_inc(part1, 1)

            def q(g, par, e):
                first_part(g, e, f"q{e}", k_out, 16 * g)

            def q_parts(g, par, e):
                second_part(g, e, f"q{e}")

            def k(g, par, e):
                first_part(g, e, f"k{e}", q_out, 16 * (g + 1))

            def k_parts(g, par, e):
                second_part(g, e, f"k{e}")

            def v(g, par, i):
                act.wait_ge(full_e, n_embed(g, f"v{i}") + 1)
                copy(vx4[par][:, 2 * i:2 * i + 2, :, 0:HD],
                     ps[6][:, :].rearrange("p (b h d) -> p b h d", b=2, d=HD)).then_inc(empty_e, 1)

            def relative(g, par, c):
                bank = rk_bank(c)
                act.wait_ge(full[bank], n_rel(g, bank, c) + 1)
                copy(rk3[:, :, RC * c:RC * (c + 1)],
                     ps[bank][:, :].rearrange("p (l n) -> p n l", n=HB)).then_inc(empty[bank], 1)

            def logits(g, par, u):
                if u % 2:
                    act.wait_ge(centred, H * g + u + 1)
                    part = rq3[:, GB * (u - 1):GB * (u + 1), :]
                    nc.scalar.activation(part, part, ACT.Exp, scale=SCALE).then_inc(exp_done, 1)

            def probT(g, par, u):
                if u % 2 == 0 or u % 4 == 1:
                    bank = 4 + u % 2
                    act.wait_ge(full[bank], n_probT(g, u) + 1)
                    copy(rk[:, TOK * u:TOK * (u + 1)], ps[bank][:, :]).then_inc(empty[bank], 1)

            def weigh(g, par, q):
                act.wait_ge(full[0], n_pv(g, q) + 1)
                act.wait_ge(full[1], n_pv(g, q))
                copy(pv[:, :], ps[0][:, :]).then_inc(empty[0], 1)

            def weigh_rel(g, par, c):
                if c % 2 == 0:
                    act.wait_ge(full[0], n_av(g, c) + 1)
                    copy(oav[:, 512 * c:512 * (c + 1)], ps[0][:, :]).then_inc(empty[0], 1)

            def turn2(g, par, c):
                act.wait_ge(full_m, n_mix(g, f"t{c}") + 1)
                copy(turned(c), ps[7][:, :].rearrange("p (b s) -> p b s", b=GB)).then_inc(empty_m, 1)

            def gate(g, par, i):
                act.wait_ge(mixed, 2 * CT * (g + 1))
                act.wait_ge(full_m, n_mix(g, f"r{i}") + 1)
                nc.scalar.activation(mrows[:, TOK * i:TOK * (i + 1)], ps[7][:, :], ACT.Tanh,
                                     scale=0.5).then_inc(empty_m, 1)

            def key(g, par, e):
                act.wait_ge(full_m, n_mix(g, f"k{e}") + 1)
                nc.scalar.activation(kact[:, e * TOK:(e + 1) * TOK], ps[7][:, :], ACT.Relu).then_inc(empty_m, 1)

            pipeline(act, dict(turn1=turn1, q=q, q_parts=q_parts, k=k, k_parts=k_parts, v=v, relative=relative,
                               logits=logits, probT=probT, weigh=weigh, weigh_rel=weigh_rel, turn2=turn2,
                               gate=gate, key=key))

        @block.vector
        def _(dve):
            vec = nc.vector
            done = [0]

            def link(ins):
                done[0] += 1
                ins.then_inc(setup_v, 1)
                dve.wait_ge(setup_v, done[0])

            def split_table(tab, x, left, rows):
                for n in range(NPART):
                    part = tab[:, n * TW:(n + 1) * TW]
                    link(vec.tensor_copy(part, x))
                    if n < NPART - 1:
                        link(vec.tensor_tensor(left, x, part, ALU.subtract))
                    x = left

            dve.wait_ge(const_in, N_CONST)
            for t in (ekf, eqf):
                link(vec.tensor_copy(t[:, 0:R - 1], t[:, R - 1:R].broadcast_to([HD, R - 1])))
                link(vec.tensor_copy(t[:, 3 * R:TW], t[:, 3 * R - 1:3 * R].broadcast_to([HD, R - 1])))
            link(vec.tensor_copy(ekr, ekf[:, ::-1]))
            link(vec.memset(ones, 1.0))
            link(vec.tensor_tensor(prod, ekf, eqf, ALU.mult))
            split_table(k_tab, ekr, rest, HD)
            split_table(q_tab, eqf, rest, HD)
            dve.wait_ge(pp_sum, 1)
            link(vec.tensor_copy(pp, ps[7][0:1, 0:TW]))
            split_table(pp_tab, pp, rest[0:1, :], 1)
            link(vec.tensor_tensor(pos0[:, :], pos0[:, :], rows[:, 0:D], ALU.add))
            link(vec.tensor_tensor(dtype_[:, :], rows[:, D:2 * D], rows[:, 0:D], ALU.subtract))
            for i in range(2):
                link(vec.memset(ks[i][KR:KR1, :], 1.0))
            assert done[0] == N_SETUP_V
            dve.wait_ge(setup_g, N_SETUP_G)

            def statistics(kind, g, src):
                for b in range(GB):
                    vec.bn_stats(bn[kind][:, 6 * b:6 * b + 6], src[:, b * D:(b + 1) * D]).then_inc(stats[kind], 1)
                for b in range(GB):
                    dve.wait_ge(stats[kind], GB * g + b + 1)
                    apart(dve)
                    vec.bn_aggr(mv[kind][:, 2 * b:2 * b + 2], bn[kind][:, 6 * b:6 * b + 6]).then_inc(meanvar[kind], 1)

            def normalise(kind, g, src, dst):
                dve.wait_ge(rstd_ready[kind], g + 1)
                for b in range(GB):
                    vec.tensor_scalar(dst[:, b * D:(b + 1) * D], src[:, b * D:(b + 1) * D],
                                      mv[kind][:, 2 * b:2 * b + 1], rstd[kind][:, b:b + 1],
                                      ALU.subtract, ALU.mult).then_inc(normed[kind], 1)

            def type_(g, par):
                dve.wait_ge(ids_in, 32 * (g + 1))
                vec.tensor_copy(tyf[:, :], tyt[:, :]).then_inc(tyf_ready, 1)
                dve.wait_ge(tyf_ready, g + 1)
                dve.wait_ge(pos_added, g + 1)
                for b in range(GB):
                    row = h[par][:, b * D:(b + 1) * D]
                    vec.scalar_tensor_tensor(row, dtype_[:, :], tyf[:, b:b + 1], row, ALU.mult, ALU.add)\
                       .then_inc(x_ready, 1)
                dve.wait_ge(x_ready, GB * (g + 1))
                statistics(0, g, h[par])

            def apply0(g, par):
                normalise(0, g, h[par], h[par])

            def stats1(g, par):
                dve.wait_ge(h_ready, g + 1)
                statistics(1, g, h[par])

            def apply1(g, par):
                if past(g):
                    dve.wait_ge(part2, 4 * g)
                normalise(1, g, h[par], rows)

            def left_over(g, e, n, use):
                dve.wait_ge(part0, 4 * g + 2 * n + e + 1)
                if n:
                    dve.wait_ge(part2, 4 * g + e + 1)
                vec.tensor_tensor(rows[:, e * TOK:(e + 1) * TOK], ps[6][:, :],
                                  parts3[:, 0, e * TOK:(e + 1) * TOK], ALU.subtract).then_inc(empty_e, 1)

            def last_part(g, e, n):
                dve.wait_ge(part1, 4 * g + 2 * n + e + 1)
                vec.tensor_tensor(parts3[:, 2, e * TOK:(e + 1) * TOK], rows[:, e * TOK:(e + 1) * TOK],
                                  parts3[:, 1, e * TOK:(e + 1) * TOK], ALU.subtract).then_inc(part2, 1)

            def q(g, par, e):
                left_over(g, e, 0, f"q{e}")

            def q_parts(g, par, e):
                last_part(g, e, 0)

            def k(g, par, e):
                left_over(g, e, 1, f"k{e}")

            def k_parts(g, par, e):
                last_part(g, e, 1)

            def relative(g, par, c):
                bank = rq_bank(c)
                dve.wait_ge(full[bank], n_rel(g, bank, c) + 1)
                vec.tensor_copy(rq3[:, :, RC * c:RC * (c + 1)],
                                ps[bank][:, :].rearrange("p (m n) -> p n m", n=HB)).then_inc(empty[bank], 1)

            def logits(g, par, u):
                bank = 2 + u % 2
                if u == 0:
                    for n in (1, 3):
                        dve.wait_ge(empty[n], n_rel(g, n, NRC))
                dve.wait_ge(full[bank], n_logit(g, u) + 1)
                apart(dve)
                for b in range(GB):
                    n = GB * u + b
                    ins = vec.tensor_tensor_reduce(out=rq3[:, n, :], in0=ps[bank][:, b * S:(b + 1) * S],
                                                   in1=rq3[:, n, :], scale=1.0, scalar=LOWEST, op0=ALU.add,
                                                   op1=ALU.max, accum_out=mx[:, n:n + 1])
                ins.then_inc(empty[bank], 1)

            def probT(g, par, u):
                if u % 4 == 3:
                    dve.wait_ge(full[5], n_probT(g, u) + 1)
                    vec.tensor_copy(rk[:, TOK * u:TOK * (u + 1)], ps[5][:, :]).then_inc(empty[5], 1)

            def turn(g, par, q):
                dve.wait_ge(full[1], n_pv(g, q) + 1)
                if q == 0 and past(g):
                    dve.wait_ge(o_sum, g)
                vec.tensor_copy(ot4[:, :, 4 * q:4 * q + 4, :],
                                ps[1][:, :].rearrange("p (b j c) -> p b j c", b=GB, j=4)[:, :, :, 0:VW])\
                   .then_inc(empty[1], 1)

            def weigh_rel(g, par, c):
                if c % 2:
                    dve.wait_ge(full[1], n_av(g, c) + 1)
                    vec.tensor_copy(oav[:, 512 * c:512 * (c + 1)], ps[1][:, :]).then_inc(empty[1], 1)

            def combine(g, par):
                dve.wait_ge(empty[1], USES[1] * (g + 1))
                vec.reciprocal(rden[:, :], ot3[:, :, HD]).then_inc(rden_ready, 1)
                dve.wait_ge(orel_in, 16 * (g + 1))
                vec.tensor_tensor(h2[:, :].rearrange("p (b h d) -> p b h d", b=GB, d=HD), ot4[:, :, :, 0:HD],
                                  orel[:, :].rearrange("p (d h b) -> p b h d", d=HD, b=GB), ALU.add)\
                   .then_inc(o_sum, 1)
                dve.wait_ge(o_sum, g + 1)
                dve.wait_ge(rden_ready, g + 1)
                n3 = h2[:, :].rearrange("p (n d) -> p n d", d=HD)
                vec.tensor_tensor(n3, n3, rden[:, :].unsqueeze(2).broadcast_to([P, HB, HD]), ALU.mult)\
                   .then_inc(o_norm, 1)

            def stats2(g, par):
                dve.wait_ge(h2_ready, g + 1)
                statistics(2, g, h2)

            def apply2(g, par):
                normalise(2, g, h2, mrows)

            def diff(g, par):
                dve.wait_ge(empty_m, n_mix(g, "t1") + 1)
                vec.tensor_tensor(mrows[:, :].rearrange("p (n s) -> p n s", s=S), nT[:, :, 1:S + 1], nT[:, :, 0:S],
                                  ALU.subtract).then_inc(diff_ready, 1)

            def mix_rows(g, dst, mu):
                dve.wait_ge(diff_ready, g + 1)
                for c in range(CT):
                    vec.scalar_tensor_tensor(
                        dst[:, c * TOK:(c + 1) * TOK].rearrange("p (b s) -> p b s", b=GB),
                        mrows[:, c * TOK:(c + 1) * TOK].rearrange("p (b s) -> p b s", b=GB), mu[:, c:c + 1],
                        nT[:, c * GB:(c + 1) * GB, 0:S], ALU.mult, ALU.add).then_inc(mixed, 1)

            def mix_r(g, par):
                mix_rows(g, xr, mur)

            def mix_k(g, par):
                mix_rows(g, xk, muk)

            def value(g, par, i):
                half = slice(TOK * i, TOK * (i + 1))
                dve.wait_ge(empty_m, n_mix(g, "r1") + 1)
                dve.wait_ge(full_m, n_mix(g, f"v{i}") + 1)
                vec.scalar_tensor_tensor(mrows[:, half], mrows[:, half], 1.0, ps[7][:, :], ALU.add, ALU.mult)\
                   .then_inc(empty_m, 1)
                dve.wait_ge(empty_m, n_mix(g, f"v{i}") + 1)
                vec.scalar_tensor_tensor(h2[:, half], mrows[:, half], 0.5, h2[:, half], ALU.mult, ALU.add)\
                   .then_inc(result, 1)

            pipeline(dve, dict(type=type_, apply0=apply0, stats1=stats1, apply1=apply1, q=q, q_parts=q_parts, k=k,
                               k_parts=k_parts, relative=relative, logits=logits, probT=probT, turn=turn,
                               weigh_rel=weigh_rel, combine=combine, stats2=stats2, apply2=apply2, diff=diff,
                               mix_r=mix_r, mix_k=mix_k, value=value))

        @block.tensor
        def _(pe):
            mm = nc.tensor.matmul
            pe.wait_ge(const_in, N_CONST)
            pe.wait_ge(setup_v, 4 + 3)
            mm(ps[7][0:1, 0:TW], ones, prod, start=True, stop=True).then_inc(pp_sum, 1)
            pe.wait_ge(setup_g, N_SETUP_G)
            pe.wait_ge(slots_in, 16 * (2 * SLOTS + NPART))

            def transpose(dst, src, **kw):
                return mm(dst, src, ident[:, :], is_transpose=True, **kw)

            def features(dst, src, c):
                for b in range(GB):
                    ins = transpose(dst[:, b * S:(b + 1) * S], src[:, b * D + c * P:b * D + (c + 1) * P],
                                    start=True, stop=True)
                return ins

            def tile_product(dst, w, e, src):
                for c in range(CT):
                    ins = mm(dst[:, :], w[:, c * D + e * P:c * D + (e + 1) * P], src(c), start=c == 0, stop=c == CT - 1)
                return ins

            def row_product(dst, w, i, src):
                for n in range(2):
                    for c in range(CT):
                        ins = mm(dst[:, n * D:(n + 1) * D], src(c, 2 * i + n), w[:, c * D:(c + 1) * D],
                                 start=c == 0, stop=c == CT - 1)
                return ins

            def turn1(g, par, c):
                pe.wait_ge(normed[1], GB * (g + 1))
                if past(g) or c:
                    pe.wait_ge(empty_e, n_embed(g, f"t{c}"))
                features(ps[6], rows, c).then_inc(full_e, 1)

            def project(g, w, e, use):
                pe.wait_ge(empty_e, n_embed(g, use))
                tile_product(ps[6], w, e, lambda c: nT[:, c * GB:(c + 1) * GB, 1:S + 1]).then_inc(full_e, 1)

            def q(g, par, e):
                project(g, w_q, e, f"q{e}")

            def k(g, par, e):
                project(g, w_k, e, f"k{e}")

            def v(g, par, i):
                pe.wait_ge(empty_e, n_embed(g, f"v{i}"))
                row_product(ps[6], w_v, i, lambda c, b: nT[:, c * GB + b, 1:S + 1]).then_inc(full_e, 1)

            def relative(g, par, c):
                if c == 0:
                    pe.wait_ge(q_in, 16 * SLOTS * (g + 1))
                    pe.wait_ge(k_in, 16 * SLOTS * (g + 1))
                bank = rk_bank(c)
                if past(g) or c > 1:
                    pe.wait_ge(empty[bank], n_rel(g, bank, c))
                for i in range(RC):
                    l = RC * c + i
                    ins = mm(ps[bank][:, i * HB:(i + 1) * HB], ekw[0:KR, S - 1 - l:TW - l], qs3[par][0:KR, :, l],
                             start=True, stop=True)
                ins.then_inc(full[bank], 1)
                bank = rq_bank(c)
                if past(g) or c > 1:
                    pe.wait_ge(empty[bank], n_rel(g, bank, c))
                for i in range(RC):
                    m = RC * c + i
                    ins = mm(ps[bank][:, i * HB:(i + 1) * HB], eqw[0:KR1, S - 1 - m:TW - m], ks3[par][0:KR1, :, m],
                             start=True, stop=True)
                ins.then_inc(full[bank], 1)

            def logits(g, par, u):
                bank = 2 + u % 2
                if u == 0:
                    for n in (0, 2):
                        pe.wait_ge(empty[n], n_rel(g, n, NRC))
                pe.wait_ge(empty[bank], n_logit(g, u))
                for b in range(GB):
                    n = GB * u + b
                    dst = ps[bank][:, b * S:(b + 1) * S]
                    mm(dst, qs3[par][0:KR, n, :], ks3[par][0:KR, n, :], start=True, stop=False)
                    ins = transpose(dst, rk3[:, n, :], start=False, stop=True)
                ins.then_inc(full[bank], 1)

            def probT(g, par, u):
                bank = 4 + u % 2
                pe.wait_ge(exp_done, H // 2 * g + u // 2 + 1)
                if past(g) or u > 1:
                    pe.wait_ge(empty[bank], n_probT(g, u))
                for b in range(GB):
                    ins = transpose(ps[bank][:, b * S:(b + 1) * S], rq3[:, GB * u + b, :], start=True, stop=True)
                ins.then_inc(full[bank], 1)

            def weigh(g, par, q):
                for n in (4, 5):
                    pe.wait_ge(empty[n], n_probT(g, 4 * q + 4))
                pe.wait_ge(empty[0], n_pv(g, q))
                if q == 0:
                    pe.wait_ge(empty_e, n_embed(g, "v1") + 1)
                for b in range(GB):
                    for j in range(4):
                        hd = 4 * q + j
                        ins = mm(ps[0][32 * j:32 * j + VW, b * S:(b + 1) * S], vx4[par][:, b, hd, :],
                                 rk3[:, GB * hd + b, :], start=True, stop=True, tile_position=(0, 32 * j))
                ins.then_inc(full[0], 1)

            def turn(g, par, q):
                pe.wait_ge(empty[0], n_pv(g, q) + 1)
                pe.wait_ge(empty[1], n_pv(g, q))
                for b in range(GB):
                    ins = transpose(ps[1][:, b * P:(b + 1) * P], pv[:, b * S:(b + 1) * S], start=True, stop=True)
                ins.then_inc(full[1], 1)

            def weigh_rel(g, par, c):
                bank = c % 2
                pe.wait_ge(empty[bank], n_av(g, c))
                for i in range(8):
                    for j in range(4):
                        l = 32 * j + 8 * c + i
                        ins = mm(ps[bank][32 * j:32 * j + HD, i * HB:(i + 1) * HB], avt[:, (S - 1 - l) * HD:(S - l) * HD],
                                 rk3[:, :, l], start=True, stop=True, tile_position=(0, 32 * j))
                ins.then_inc(full[bank], 1)

            def turn2(g, par, c):
                pe.wait_ge(normed[2], GB * (g + 1))
                if isinstance(g, int) or c:
                    pe.wait_ge(empty_m, n_mix(g, f"t{c}"))
                features(ps[7], mrows, c).then_inc(full_m, 1)

            def gate(g, par, i):
                pe.wait_ge(mixed, 2 * CT * g + CT)
                pe.wait_ge(empty_m, n_mix(g, f"r{i}"))
                row_product(ps[7], w_r, i, lambda c, b: xr[:, c * TOK + b * S:c * TOK + (b + 1) * S])\
                    .then_inc(full_m, 1)

            def key(g, par, e):
                pe.wait_ge(mixed, 2 * CT * (g + 1))
                pe.wait_ge(empty_m, n_mix(g, f"k{e}"))
                tile_product(ps[7], w_fk, e, lambda c: xk[:, c * TOK:(c + 1) * TOK]).then_inc(full_m, 1)

            def value(g, par, i):
                pe.wait_ge(squared, CT * (g + 1))
                pe.wait_ge(empty_m, n_mix(g, f"v{i}"))
                row_product(ps[7], w_fv, i, lambda c, b: kact[:, c * TOK + b * S:c * TOK + (b + 1) * S])\
                    .then_inc(full_m, 1)

            pipeline(pe, dict(turn1=turn1, q=q, k=k, v=v, relative=relative, logits=logits, probT=probT,
                              weigh=weigh, turn=turn, weigh_rel=weigh_rel, turn2=turn2, gate=gate, key=key,
                              value=value))


_INS = ['ids', 'types', 'word', 'pos', 'typ', 'gamma', 'beta', 'wq', 'wk', 'wv', 'eq', 'ek', 'ev',
        'wr_t', 'wk_t', 'wv_t', 'mu_r', 'mu_k']


def kernel(**inputs):
    import numpy as np
    import concourse.bacc as bacc
    from concourse.bass_utils import run_bass_kernel_spmd

    x = {k: np.asarray(v) for k, v in inputs.items()}

    def by_group(a):
        return a.reshape(NG, GB, S).transpose(0, 2, 1)

    data = dict(
        ids=by_group(x['x']), types=by_group(x['mask_BS_i1_0']), word=x['L0_tok_word_emb'],
        pos=x['L0_tok_pos_emb'], typ=x['L0_tok_type_emb'], gamma=x['L0_tok_gamma'], beta=x['L0_tok_beta'],
        wq=x['L0_attn_Wq'], wk=x['L0_attn_Wk'], wv=x['L0_attn_Wv'], eq=x['L0_attn_Eq'].T, ek=x['L0_attn_Ek'].T,
        ev=x['L0_attn_Ev'][::-1], wr_t=x['L0_ffn_W_r'].T, wk_t=x['L0_ffn_W_k'].T, wv_t=x['L0_ffn_W_v'].T,
        mu_r=x['L0_ffn_mu_r'].reshape(CT, P).T, mu_k=x['L0_ffn_mu_k'].reshape(CT, P).T)
    nc = bacc.Bacc("TRN2", target_bir_lowering=False, num_devices=1, dynamic_dma_scratch_size=8192)
    arrays, args = {}, []
    for name in _INS:
        a = np.ascontiguousarray(data[name])
        arrays[f"in_{name}"] = a
        args.append(nc.dram_tensor(f"in_{name}", a.shape, mybir.dt.from_np(a.dtype), kind="ExternalInput").ap())
    out = nc.dram_tensor("out", (B, S, D), fp32, kind="ExternalOutput").ap()
    tower_kernel(nc, *args, out.rearrange("(g b) s n -> g s b n", b=GB))
    r = run_bass_kernel_spmd(nc, [arrays], core_ids=[0])
    return r.results[0]["out"]
```

```python
import concourse.bass as bass
from concourse import mybir
from contextlib import ExitStack

fp32 = mybir.dt.float32
bf16 = mybir.dt.bfloat16
i32 = mybir.dt.int32
ALU = mybir.AluOpType
ACT = mybir.ActivationFunctionType

P = 128
B, S, D = 128, 128, 256
H, HD = 16, 16
R = 64
GB = 4
NG = B // GB
TOK = GB * S
HB = H * GB
CT = D // P
NPART = 3
SLOTS = 6
TW = 2 * S - 1
VW = HD + 1
Q_PART = (0, 0, 0, 1, 1, 2)
K_PART = (0, 1, 2, 0, 1, 0)
KR = SLOTS * HD
KR1 = KR + NPART
RC = 8
NRC = S // RC
LAG = 4
RQ_ON_SCALAR = (1, 4, 7, 10, 11, 12, 15)
SCALE = 1.0 / HD ** 0.5
LOWEST = -3.4028234e38
EPS_EMBED, EPS_NORM = 1e-12, 1e-5


def tower_kernel(nc, ids, types, word, pos, typ, gamma, beta, wq, wk, wv, eq, ek, ev,
                 wr_t, wk_t, wv_t, mu_r, mu_k, out):
    ctx = ExitStack()
    with ctx:
        def sb(name, shape, dt=fp32):
            return ctx.enter_context(nc.sbuf_tensor(name, shape, dt))

        def sem(name):
            return ctx.enter_context(nc.semaphore(name))

        rk = sb("rk", [P, HB * S])
        rq = sb("rq", [P, HB * S])
        qs = [sb(f"qs{i}", [P, HB * S], bf16) for i in range(2)]
        ks = [sb(f"ks{i}", [P, HB * S], bf16) for i in range(2)]
        vx = sb("vx", [P, GB * H * VW])
        h = [sb(f"h{i}", [P, GB * D]) for i in range(2)]
        h2 = sb("h2", [P, GB * D])
        rows = sb("rows", [P, GB * D])
        mrows = sb("mrows", [P, GB * D])
        normT = sb("normT", [P, CT * GB * (S + 1)])
        parts = sb("parts", [P, NPART * CT * TOK], bf16)
        pv = sb("pv", [P, TOK])
        ot = sb("ot", [P, HB * VW])
        orel = sb("orel", [P, HD * HB])
        xrk = sb("xrk", [P, 2 * CT * TOK])
        xr, xk = xrk[:, 0:CT * TOK], xrk[:, CT * TOK:]
        kact = xr
        oav = xrk
        avt = sb("avt", [P, S * HD])
        ekw = sb("ekw", [P, TW], bf16)
        eqw = sb("eqw", [P, TW], bf16)
        w_q, w_k, w_v, w_r, w_fk, w_fv = (sb(n, [P, CT * D]) for n in
                                          ("w_q", "w_k", "w_v", "w_r", "w_fk", "w_fv"))
        ident = sb("ident", [P, P])
        pos0 = sb("pos0", [P, D])
        dtype_ = sb("dtype_", [P, D])
        gam = sb("gam", [P, D])
        bet = sb("bet", [P, D])
        mur = sb("mur", [P, CT])
        muk = sb("muk", [P, CT])
        omur = sb("omur", [P, CT])
        omuk = sb("omuk", [P, CT])
        neghalf = sb("neghalf", [P, GB])
        idt = sb("idt", [P, GB], i32)
        tyt = sb("tyt", [P, GB], i32)
        tyf = sb("tyf", [P, GB])
        bn = [sb(f"bn{i}", [P, GB * 6]) for i in range(3)]
        mv = [sb(f"mv{i}", [P, GB * 2]) for i in range(3)]
        rstd = [sb(f"rstd{i}", [P, GB]) for i in range(3)]
        mx = sb("mx", [P, HB])
        rden = sb("rden", [P, HB])
        ekf = rk[0:HD, 0:TW]
        ekr = rk[0:HD, TW:2 * TW]
        eqf = rk[0:HD, 2 * TW:3 * TW]
        prod = rk[0:HD, 3 * TW:4 * TW]
        rest = rk[0:HD, 4 * TW:5 * TW]
        ones = rk[0:HD, 5 * TW:5 * TW + 1]
        pp = rk[0:1, 6 * TW:7 * TW]
        k_tab = qs[0][0:HD, 0:NPART * TW]
        q_tab = qs[1][0:HD, 0:NPART * TW]
        pp_tab = ks[0][0:1, 0:NPART * TW]

        ps = [ctx.enter_context(nc.psum_tensor(f"ps{i}", [P, 512], fp32)) for i in range(8)]

        ev_wide = nc.dram_tensor("ev_wide", [TW, HD], fp32, kind="Internal")
        q_dram = nc.dram_tensor("q_dram", [NPART, D, TOK], bf16, kind="Internal").ap()
        k_dram = nc.dram_tensor("k_dram", [NPART, D, TOK], bf16, kind="Internal").ap()
        o_dram = nc.dram_tensor("o_dram", [4, 8, P, HB], fp32, kind="Internal").ap()

        rk3 = rk[:, :].rearrange("p (n l) -> p n l", l=S)
        rq3 = rq[:, :].rearrange("p (n m) -> p n m", m=S)
        qs3 = [t[:, :].rearrange("p (n l) -> p n l", l=S) for t in qs]
        ks3 = [t[:, :].rearrange("p (n l) -> p n l", l=S) for t in ks]
        vx4 = vx[:, :].rearrange("p (b h c) -> p b h c", b=GB, c=VW)
        nT = normT[:, :].rearrange("p (n s) -> p n s", s=S + 1)
        parts3 = parts[:, :].rearrange("p (k t) -> p k t", k=NPART)
        ot3 = ot[:, :].rearrange("p (n c) -> p n c", c=VW)
        ot4 = ot[:, :].rearrange("p (b h c) -> p b h c", b=GB, c=VW)

        const_in = sem("const_in")
        setup_v = sem("setup_v")
        setup_g = sem("setup_g")
        pp_sum = sem("pp_sum")
        slots_in = sem("slots_in")
        wide_out = sem("wide_out")
        full = [sem(f"full{i}") for i in range(6)]
        empty = [sem(f"empty{i}") for i in range(6)]
        full_e = sem("full_e")
        empty_e = sem("empty_e")
        full_m = sem("full_m")
        empty_m = sem("empty_m")
        ids_in = sem("ids_in")
        words_in = sem("words_in")
        pos_added = sem("pos_added")
        tyf_ready = sem("tyf_ready")
        x_ready = sem("x_ready")
        stats = [sem(f"stats{i}") for i in range(3)]
        meanvar = [sem(f"meanvar{i}") for i in range(3)]
        eps_added = [sem(f"eps_added{i}") for i in range(3)]
        rstd_ready = [sem(f"rstd_ready{i}") for i in range(3)]
        normed = [sem(f"normed{i}") for i in range(3)]
        scaled = sem("scaled")
        h_ready = sem("h_ready")
        part0 = sem("part0")
        part1 = sem("part1")
        part2 = sem("part2")
        q_out = [sem(f"q_out{e}") for e in range(CT)]
        k_out = [sem(f"k_out{e}") for e in range(CT)]
        q_in = sem("q_in")
        k_in = sem("k_in")
        centred = sem("centred")
        exp_done = sem("exp_done")
        oav_out = sem("oav_out")
        orel_in = sem("orel_in")
        rden_ready = sem("rden_ready")
        o_sum = sem("o_sum")
        h2_ready = sem("h2_ready")
        o_norm = sem("o_norm")
        mixed = sem("mixed")
        k_scaled = sem("k_scaled")
        squared = sem("squared")
        result = sem("result")
        stored = sem("stored")
        passed = sem("passed")

        N_CONST = 16 * (6 + 5 + 2 + 2 + 1)
        N_SETUP_G = 7
        N_SETUP_V = 4 + 3 + 3 * 5 + 1 + 2 + 2
        EPS = (EPS_EMBED, EPS_NORM, EPS_NORM)

        RELATIVE_USES = (6, 6, 5, 5, 5, 5)
        USES = (10, 10, 14, 14, 14, 14)
        AV_BANK = (4, 5, 2, 3)
        EMBED_USES = ("t0", "t1", "q0", "q1", "k0", "k1", "v0", "v1")
        MIX_USES = ("t0", "t1", "r0", "r1", "k0", "k1", "v0", "v1")

        def n_rel(g, bank, c):
            return g * USES[bank] + c // 3

        def n_logit(g, u):
            return g * USES[2] + RELATIVE_USES[2] + u // 2

        def n_probT(g, u):
            return g * USES[4] + RELATIVE_USES[4] + u // 2

        def n_pv(g, q):
            return g * USES[0] + RELATIVE_USES[0] + q

        def n_av(g, c):
            return (g + 1) * USES[AV_BANK[c]] - 1

        def n_embed(g, use):
            return g * len(EMBED_USES) + EMBED_USES.index(use)

        def n_mix(g, use):
            return g * len(MIX_USES) + MIX_USES.index(use)

        def rk_bank(c):
            return (0, 4, 2)[c % 3]

        def rq_bank(c):
            return (1, 5, 3)[c % 3]

        def past(g, n=1):
            return not isinstance(g, int) or g >= n

        def apart(eng):
            eng.sem_inc(passed, 1)

        MIX_AT = ((10, "combine"), (10, "residual"), (15, "stats2"), (15, "root2"), (17, "apply2"),
                  (17, "turn2", 0), (18, "turn2_out", 0), (18, "turn2", 1), (19, "turn2_out", 1),
                  (19, "mix_r"), (20, "scale_k"), (22, "mix_k"),
                  (19, "gate", 0), (20, "gate_out", 0), (21, "gate", 1), (22, "gate_out", 1),
                  (26, "key", 0), (27, "key_out", 0), (28, "square", 0), (29, "key", 1), (30, "key_out", 1),
                  (30, "square", 1),
                  (32, "value", 0), (33, "value_out", 0), (33, "value", 1), (34, "value_out", 1), (35, "store"))
        VALUES_AT = ((15, "v", 0), (16, "v_out", 0), (16, "v", 1), (17, "v_out", 1))
        EMBED_AT = ((4, "apply0"), (15, "gamma"), (18, "beta"), (20, "stats1"), (20, "root1"), (22, "apply1"),
                    (22, "turn1", 0), (23, "turn1_out", 0), (23, "turn1", 1), (24, "turn1_out", 1),
                    (24, "q", 0), (25, "q_out", 0), (26, "q_parts", 0), (25, "q", 1), (26, "q_out", 1), (27, "q_parts", 1),
                    (27, "k", 0), (28, "k_out", 0), (29, "k_parts", 0), (28, "k", 1), (29, "k_out", 1), (30, "k_parts", 1))
        ROWS_AT = ((28, "fetch"), (31, "gather", 0), (32, "gather", 1), (34, "gather", 2), (35, "gather", 3),
                   (37, "position"), (38, "type"), (39, "stats0"), (40, "root0"))

        STEPS_AT = dict(mix=MIX_AT, values=VALUES_AT, embed=EMBED_AT, rows=ROWS_AT)
        AHEAD = {x[1]: d for what, d in (("mix", -1), ("values", 0), ("embed", 1), ("rows", 2)) for x in STEPS_AT[what]}
        PRODUCTS = ("turn2", "gate", "key", "value", "turn1", "q", "k", "v")

        def order(*kinds):
            attend = "attend" in kinds
            steps = []
            for slot in range(NRC + H + LAG + 5):
                here = [tuple(x) for kind, steps_at in STEPS_AT.items() for at, *x in steps_at
                        if kind in kinds and at == slot]
                u = slot - NRC
                v, c = u - LAG, u - LAG - H
                early = [x for x in here if x[0] == "turn2_out"]
                steps += early
                if attend and u >= 0:
                    if u % 2 and 3 <= u < H + 3:
                        steps.append(("exp", (u - 3) // 2))
                    if 0 < u <= H:
                        steps.append(("centre", u - 1))
                    if 0 < v <= H:
                        steps.append(("prob_out", v - 1))
                    if v >= 5 and v % 4 == 1:
                        steps.append(("weigh_out", v // 4 - 1))
                    if v >= 6 and v % 4 == 2:
                        steps.append(("turn_out", v // 4 - 1))
                    if c > 0:
                        steps.append(("weigh_rel_out", c - 1))
                steps += [x for x in here if x[0] not in PRODUCTS and x not in early]
                if attend:
                    if u < 0:
                        steps.append(("relative", slot))
                    elif u < H:
                        steps.append(("logits", u))
                    if 0 <= v < H:
                        steps.append(("probT", v))
                    if v >= 4 and v % 4 == 0 and v <= H:
                        steps.append(("weigh", v // 4 - 1))
                    if v >= 5 and v % 4 == 1:
                        steps.append(("turn", v // 4 - 1))
                    if 0 <= c < 4:
                        steps.append(("weigh_rel", c))
                steps += [x for x in here if x[0] in PRODUCTS]
            return steps

        def run(steps, table, g):
            for name, *arg in steps:
                if name in table:
                    d = AHEAD.get(name, 0)
                    table[name](g[0] + d, (g[1] + d) % 2, *arg)

        def first_rows(table):
            run(order("rows"), table, (-2, 0))

        def pipeline(eng, table):
            everything = order("rows", "embed", "values", "attend", "mix")
            run(order("rows", "embed"), table, (-1, 1))
            run(order("rows", "embed", "values", "attend"), table, (0, 0))
            with eng.Fori(0, NG // 2 - 2) as t:
                for i in (1, 2):
                    run(everything, table, (t * 2 + i, i % 2))
            run(everything, table, (NG - 3, 1))
            run(order("embed", "values", "attend", "mix"), table, (NG - 2, 0))
            run(order("values", "attend", "mix"), table, (NG - 1, 1))
            run(order("mix"), table, (NG, 0))

        block = ctx.enter_context(nc.Block())

        @block.sync
        def _(sp):
            def load(dst, src):
                sp.dma_start(dst, src).then_inc(const_in, 16)

            def fetch(g, par):
                if past(g):
                    sp.wait_ge(words_in, 16 * GB * g)
                    sp.wait_ge(tyf_ready, g)
                    apart(sp)
                sp.dma_start(idt[:, :], ids[g]).then_inc(ids_in, 16)
                sp.dma_start(tyt[:, :], types[g]).then_inc(ids_in, 16)

            first_rows(dict(fetch=fetch))

            for dst, src in ((w_q, wq), (w_k, wk), (w_v, wv), (w_r, wr_t), (w_fk, wk_t), (w_fv, wv_t)):
                load(dst[:, :].rearrange("p (c n) -> p c n", c=CT), src.rearrange("(c p) n -> p c n", p=P))
            load(pos0[:, :], pos)
            load(gam[:, :], bass.AP(gamma.tensor, 0, [[0, P], [1, D]]))
            load(bet[:, :], bass.AP(beta.tensor, 0, [[0, P], [1, D]]))
            load(mur[:, :], mu_r)
            load(muk[:, :], mu_k)
            load(rows[:, 0:D], bass.AP(typ.tensor, 0, [[0, P], [1, D]]))
            load(rows[:, D:2 * D], bass.AP(typ.tensor, D, [[0, P], [1, D]]))
            load(ekf[:, R - 1:3 * R], ek)
            load(eqf[:, R - 1:3 * R], eq)
            wide = ev_wide.ap()
            sp.dma_start(wide[0:R - 1, :], bass.AP(ev.tensor, 0, [[0, R - 1], [1, HD]])).then_inc(wide_out, 16)
            sp.dma_start(wide[R - 1:3 * R, :], ev).then_inc(wide_out, 16)
            sp.dma_start(wide[3 * R:TW, :], bass.AP(ev.tensor, 2 * R * HD, [[0, R - 1], [1, HD]])).then_inc(wide_out, 16)
            sp.wait_ge(wide_out, 48)
            load(avt[:, :], bass.AP(ev_wide, 0, [[HD, P], [1, S * HD]]))
            sp.wait_ge(setup_v, N_SETUP_V)
            for s in range(SLOTS):
                sp.dma_start(ekw[s * HD:(s + 1) * HD, :], k_tab[:, K_PART[s] * TW:(K_PART[s] + 1) * TW]).then_inc(slots_in, 16)
                sp.dma_start(eqw[s * HD:(s + 1) * HD, :], q_tab[:, Q_PART[s] * TW:(Q_PART[s] + 1) * TW]).then_inc(slots_in, 16)
            for s in range(NPART):
                sp.dma_start(eqw[KR + s:KR + s + 1, :], pp_tab[:, s * TW:(s + 1) * TW]).then_inc(slots_in, 16)
            sp.wait_ge(slots_in, 16 * (2 * SLOTS + NPART))

            def parts_to_dram(g, e, dram, n_parts, out_done, in_done):
                if e == 0 and past(g):
                    sp.wait_ge(in_done, 16 * SLOTS * g)
                    apart(sp)
                sp.wait_ge(part2, n_parts)
                sp.dma_start(dram.rearrange("k (c p) t -> c p k t", p=P)[e],
                             parts3[:, :, e * TOK:(e + 1) * TOK]).then_inc(out_done[e], 16)

            def parts_to_slots(g, dram, slots, part_of, out_done, in_done):
                for e in range(CT):
                    sp.wait_ge(out_done[e], 16 * (g + 1))
                for s in range(SLOTS):
                    sp.dma_start(slots[s * HD:(s + 1) * HD, :].rearrange("p (n t) -> p n t", t=TOK),
                                 dram[part_of[s]].rearrange("(n d) t -> d n t", d=HD)).then_inc(in_done, 16)

            def q_parts(g, par, e):
                parts_to_dram(g, e, q_dram, 4 * g + e + 1, q_out, q_in)
                if e == 1:
                    parts_to_slots(g, q_dram, qs[par], Q_PART, q_out, q_in)

            def k_parts(g, par, e):
                parts_to_dram(g, e, k_dram, 4 * g + 2 + e + 1, k_out, k_in)
                if e == 1:
                    parts_to_slots(g, k_dram, ks[par], K_PART, k_out, k_in)

            def weigh_rel_out(g, par, c):
                if c == 0 and past(g):
                    sp.wait_ge(orel_in, 16 * g)
                    apart(sp)
                sp.wait_ge(empty[AV_BANK[c]], n_av(g, c) + 1)
                apart(sp)
                sp.dma_start(o_dram[c].rearrange("i p n -> p i n"),
                             oav[:, 512 * c:512 * (c + 1)].rearrange("p (i n) -> p i n", n=HB)).then_inc(oav_out, 16)
                if c == 3:
                    sp.wait_ge(oav_out, 64 * (g + 1))
                    if past(g):
                        sp.wait_ge(o_sum, g)
                        apart(sp)
                        sp.wait_ge(stored, 16 * g)
                        apart(sp)
                    sp.dma_start(orel[:, :], bass.AP(o_dram.tensor, 0, [[32 * HB, 4], [P * HB, 32], [1, HD * HB]]))\
                      .then_inc(orel_in, 16)

            def store(g, par):
                sp.wait_ge(result, 2 * (g + 1))
                apart(sp)
                sp.dma_start(out[g], h2[:, :].rearrange("p (b n) -> p b n", b=GB)).then_inc(stored, 16)

            pipeline(sp, dict(fetch=fetch, q_parts=q_parts, k_parts=k_parts, weigh_rel_out=weigh_rel_out, store=store))
            sp.wait_ge(stored, 16 * NG)

        @block.gpsimd
        def _(pool):
            gps = nc.gpsimd
            gps.memset(ident[:, :], 0.0).then_inc(setup_g, 1)
            pool.wait_ge(setup_g, 1)
            gps.affine_select(out=ident[:, :], in_=ident[:, :], compare_op=ALU.not_equal, fill=1.0, base=0,
                              pattern=[[-1, P]], channel_multiplier=1).then_inc(setup_g, 1)
            gps.memset(neghalf[:, :], -0.5).then_inc(setup_g, 1)
            gps.memset(normT[:, :], 0.0).then_inc(setup_g, 1)
            gps.memset(vx[:, :], 1.0).then_inc(setup_g, 1)
            pool.wait_ge(setup_g, 5)
            for i in range(2):
                gps.memset(ks[i][KR:KR1, :], 1.0).then_inc(setup_g, 1)
            pool.wait_ge(setup_g, N_SETUP_G)
            pool.wait_ge(const_in, N_CONST)
            pool.wait_ge(setup_v, N_SETUP_V)

            def inverse_root(kind, g):
                pool.wait_ge(meanvar[kind], GB * (g + 1))
                apart(pool)
                gps.tensor_scalar(rstd[kind][:, :], mv[kind][:, 1::2], EPS[kind], None, ALU.add).then_inc(eps_added[kind], 1)
                pool.wait_ge(eps_added[kind], g + 1)
                gps.tensor_tensor(rstd[kind][:, :], rstd[kind][:, :], neghalf[:, :], ALU.pow).then_inc(rstd_ready[kind], 1)

            rows3 = rows[:, :].rearrange("p (b n) -> p b n", b=GB)

            def gather(g, par, b):
                if b == 0:
                    pool.wait_ge(ids_in, 32 * (g + 1))
                    if past(g):
                        pool.wait_ge(part2, 4 * g)
                        apart(pool)
                gps.indirect_dma_start(rows[:, b * D:(b + 1) * D], None, word,
                                       bass.IndirectOffsetOnAxis(ap=idt[:, b:b + 1], axis=0)).then_inc(words_in, 16)

            def position(g, par):
                pool.wait_ge(words_in, 16 * GB * (g + 1))
                gps.tensor_tensor(rows3, rows3, pos0[:, :].unsqueeze(1).broadcast_to([P, GB, D]), ALU.add)\
                   .then_inc(pos_added, 1)

            def gamma_(g, par):
                pool.wait_ge(normed[0], GB * (g + 1))
                if past(g, 2):
                    pool.wait_ge(h2_ready, g - 1)
                h3 = h[par][:, :].rearrange("p (b n) -> p b n", b=GB)
                gps.tensor_tensor(h3, rows3, gam[:, :].unsqueeze(1).broadcast_to([P, GB, D]), ALU.mult).then_inc(scaled, 1)

            def beta_(g, par):
                pool.wait_ge(scaled, g + 1)
                h3 = h[par][:, :].rearrange("p (b n) -> p b n", b=GB)
                gps.tensor_tensor(h3, h3, bet[:, :].unsqueeze(1).broadcast_to([P, GB, D]), ALU.add).then_inc(h_ready, 1)

            def centre(g, par, u):
                pool.wait_ge(empty[2 + u % 2], n_logit(g, u) + 1)
                part = rq3[:, GB * u:GB * (u + 1), :]
                gps.tensor_tensor(part, part, mx[:, GB * u:GB * (u + 1)].unsqueeze(2).broadcast_to([P, GB, S]),
                                  ALU.subtract).then_inc(centred, 1)

            def residual(g, par):
                pool.wait_ge(o_norm, g + 1)
                gps.tensor_tensor(h2[:, :], h2[:, :], h[par][:, :], ALU.add).then_inc(h2_ready, 1)

            def square(g, par, e):
                pool.wait_ge(empty_m, n_mix(g, f"k{e}") + 1)
                t = kact[:, e * TOK:(e + 1) * TOK]
                gps.tensor_tensor(t, t, t, ALU.mult).then_inc(squared, 1)

            steps = dict(gather=gather, position=position, root0=lambda g, par: inverse_root(0, g),
                         gamma=gamma_, beta=beta_, root1=lambda g, par: inverse_root(1, g), centre=centre,
                         residual=residual, root2=lambda g, par: inverse_root(2, g), square=square)
            first_rows(steps)
            pipeline(pool, steps)

        @block.scalar
        def _(act):
            act.wait_ge(setup_g, N_SETUP_G)

            def copy(dst, src):
                return nc.scalar.activation(dst, src, ACT.Copy)

            def turned(c):
                return nT[:, c * GB:(c + 1) * GB, 1:S + 1]

            def turn1_out(g, par, c):
                act.wait_ge(full_e, n_embed(g, f"t{c}") + 1)
                if past(g, 2):
                    act.wait_ge(mixed, 2 * CT * (g - 1))
                copy(turned(c), ps[6][:, :].rearrange("p (b s) -> p b s", b=GB)).then_inc(empty_e, 1)

            def first_part(g, e, use, out_done, n_out):
                act.wait_ge(full_e, n_embed(g, use) + 1)
                if not isinstance(n_out, int) or n_out > 0:
                    act.wait_ge(out_done[e], n_out)
                copy(parts3[:, 0, e * TOK:(e + 1) * TOK], ps[6][:, :]).then_inc(part0, 1)

            def second_part(g, e, use):
                act.wait_ge(empty_e, n_embed(g, use) + 1)
                copy(parts3[:, 1, e * TOK:(e + 1) * TOK], rows[:, e * TOK:(e + 1) * TOK]).then_inc(part1, 1)

            def q_out_(g, par, e):
                first_part(g, e, f"q{e}", k_out, 16 * g)

            def q_parts(g, par, e):
                second_part(g, e, f"q{e}")

            def k_out_(g, par, e):
                first_part(g, e, f"k{e}", q_out, 16 * (g + 1))

            def k_parts(g, par, e):
                second_part(g, e, f"k{e}")

            def v_out(g, par, i):
                act.wait_ge(full_e, n_embed(g, f"v{i}") + 1)
                copy(vx4[:, 2 * i:2 * i + 2, :, 0:HD],
                     ps[6][:, :].rearrange("p (b h d) -> p b h d", b=2, d=HD)).then_inc(empty_e, 1)

            def relative(g, par, c):
                bank = rk_bank(c)
                act.wait_ge(full[bank], n_rel(g, bank, c) + 1)
                copy(rk3[:, :, RC * c:RC * (c + 1)],
                     ps[bank][:, :].rearrange("p (l n) -> p n l", n=HB)).then_inc(empty[bank], 1)
                if c in RQ_ON_SCALAR:
                    bank = rq_bank(c)
                    act.wait_ge(full[bank], n_rel(g, bank, c) + 1)
                    copy(rq3[:, :, RC * c:RC * (c + 1)],
                         ps[bank][:, :].rearrange("p (m n) -> p n m", n=HB)).then_inc(empty[bank], 1)

            def exp(g, par, n):
                act.wait_ge(centred, H * g + 2 * n + 2)
                part = rq3[:, GB * 2 * n:GB * (2 * n + 2), :]
                nc.scalar.activation(part, part, ACT.Exp, scale=SCALE).then_inc(exp_done, 1)

            def prob_out(g, par, u):
                bank = 4 + u % 2
                act.wait_ge(full[bank], n_probT(g, u) + 1)
                copy(rk[:, TOK * u:TOK * (u + 1)], ps[bank][:, :]).then_inc(empty[bank], 1)

            def weigh_out(g, par, q):
                act.wait_ge(full[0], n_pv(g, q) + 1)
                act.wait_ge(full[1], n_pv(g, q))
                copy(pv[:, :], ps[0][:, :]).then_inc(empty[0], 1)

            def weigh_rel_out(g, par, c):
                bank = AV_BANK[c]
                act.wait_ge(full[bank], n_av(g, c) + 1)
                copy(oav[:, 512 * c:512 * (c + 1)], ps[bank][:, :]).then_inc(empty[bank], 1)

            def turn2_out(g, par, c):
                act.wait_ge(full_m, n_mix(g, f"t{c}") + 1)
                copy(turned(c), ps[7][:, :].rearrange("p (b s) -> p b s", b=GB))
                nc.scalar.activation(xr[:, c * TOK:(c + 1) * TOK], ps[7][:, :], ACT.Copy, scale=mur[:, c:c + 1])\
                    .then_inc(empty_m, 1)

            def scale_k(g, par):
                act.wait_ge(empty_m, n_mix(g, "t1") + 1)
                for c in range(CT):
                    nc.scalar.activation(xk[:, c * TOK:(c + 1) * TOK].rearrange("p (b s) -> p b s", b=GB), turned(c),
                                         ACT.Copy, scale=muk[:, c:c + 1]).then_inc(k_scaled, 1)

            def gate_out(g, par, i):
                act.wait_ge(full_m, n_mix(g, f"r{i}") + 1)
                nc.scalar.activation(mrows[:, TOK * i:TOK * (i + 1)], ps[7][:, :], ACT.Tanh,
                                     scale=0.5).then_inc(empty_m, 1)

            def key_out(g, par, e):
                act.wait_ge(full_m, n_mix(g, f"k{e}") + 1)
                nc.scalar.activation(kact[:, e * TOK:(e + 1) * TOK], ps[7][:, :], ACT.Relu).then_inc(empty_m, 1)

            steps = dict(turn1_out=turn1_out, q_out=q_out_, q_parts=q_parts, k_out=k_out_, k_parts=k_parts,
                         v_out=v_out, relative=relative, exp=exp, prob_out=prob_out, weigh_out=weigh_out,
                         weigh_rel_out=weigh_rel_out, turn2_out=turn2_out, scale_k=scale_k,
                         gate_out=gate_out, key_out=key_out)
            first_rows(steps)
            pipeline(act, steps)

        @block.vector
        def _(dve):
            vec = nc.vector
            done = [0]

            def link(ins):
                done[0] += 1
                ins.then_inc(setup_v, 1)
                dve.wait_ge(setup_v, done[0])

            def split_table(tab, x, left, rows):
                for n in range(NPART):
                    part = tab[:, n * TW:(n + 1) * TW]
                    link(vec.tensor_copy(part, x))
                    if n < NPART - 1:
                        link(vec.tensor_tensor(left, x, part, ALU.subtract))
                    x = left

            dve.wait_ge(const_in, N_CONST)
            for t in (ekf, eqf):
                link(vec.tensor_copy(t[:, 0:R - 1], t[:, R - 1:R].broadcast_to([HD, R - 1])))
                link(vec.tensor_copy(t[:, 3 * R:TW], t[:, 3 * R - 1:3 * R].broadcast_to([HD, R - 1])))
            link(vec.tensor_copy(ekr, ekf[:, ::-1]))
            link(vec.memset(ones, 1.0))
            link(vec.tensor_tensor(prod, ekf, eqf, ALU.mult))
            split_table(k_tab, ekr, rest, HD)
            split_table(q_tab, eqf, rest, HD)
            dve.wait_ge(pp_sum, 1)
            link(vec.tensor_copy(pp, ps[7][0:1, 0:TW]))
            split_table(pp_tab, pp, rest[0:1, :], 1)
            link(vec.tensor_tensor(pos0[:, :], pos0[:, :], rows[:, 0:D], ALU.add))
            link(vec.tensor_tensor(dtype_[:, :], rows[:, D:2 * D], rows[:, 0:D], ALU.subtract))
            for one_less, mu in ((omur, mur), (omuk, muk)):
                link(vec.tensor_scalar(one_less[:, :], mu[:, :], -1.0, 1.0, ALU.mult, ALU.add))
            assert done[0] == N_SETUP_V
            dve.wait_ge(setup_g, N_SETUP_G)

            def statistics(kind, g, src):
                for b in range(GB):
                    vec.bn_stats(bn[kind][:, 6 * b:6 * b + 6], src[:, b * D:(b + 1) * D]).then_inc(stats[kind], 1)
                for b in range(GB):
                    dve.wait_ge(stats[kind], GB * g + b + 1)
                    apart(dve)
                    vec.bn_aggr(mv[kind][:, 2 * b:2 * b + 2], bn[kind][:, 6 * b:6 * b + 6]).then_inc(meanvar[kind], 1)

            def normalise(kind, g, src, dst):
                dve.wait_ge(rstd_ready[kind], g + 1)
                for b in range(GB):
                    vec.tensor_scalar(dst[:, b * D:(b + 1) * D], src[:, b * D:(b + 1) * D],
                                      mv[kind][:, 2 * b:2 * b + 1], rstd[kind][:, b:b + 1],
                                      ALU.subtract, ALU.mult).then_inc(normed[kind], 1)

            def type_(g, par):
                dve.wait_ge(ids_in, 32 * (g + 1))
                vec.tensor_copy(tyf[:, :], tyt[:, :]).then_inc(tyf_ready, 1)
                dve.wait_ge(tyf_ready, g + 1)
                dve.wait_ge(pos_added, g + 1)
                for b in range(GB):
                    row = rows[:, b * D:(b + 1) * D]
                    vec.scalar_tensor_tensor(row, dtype_[:, :], tyf[:, b:b + 1], row, ALU.mult, ALU.add)\
                       .then_inc(x_ready, 1)

            def stats0(g, par):
                dve.wait_ge(x_ready, GB * (g + 1))
                statistics(0, g, rows)

            def apply0(g, par):
                normalise(0, g, rows, rows)

            def stats1(g, par):
                dve.wait_ge(h_ready, g + 1)
                statistics(1, g, h[par])

            def apply1(g, par):
                normalise(1, g, h[par], rows)

            def left_over(g, e, n, use):
                dve.wait_ge(part0, 4 * g + 2 * n + e + 1)
                if n:
                    dve.wait_ge(part2, 4 * g + e + 1)
                vec.tensor_tensor(rows[:, e * TOK:(e + 1) * TOK], ps[6][:, :],
                                  parts3[:, 0, e * TOK:(e + 1) * TOK], ALU.subtract).then_inc(empty_e, 1)

            def last_part(g, e, n):
                dve.wait_ge(part1, 4 * g + 2 * n + e + 1)
                vec.tensor_tensor(parts3[:, 2, e * TOK:(e + 1) * TOK], rows[:, e * TOK:(e + 1) * TOK],
                                  parts3[:, 1, e * TOK:(e + 1) * TOK], ALU.subtract).then_inc(part2, 1)

            def q_out_(g, par, e):
                left_over(g, e, 0, f"q{e}")

            def q_parts(g, par, e):
                last_part(g, e, 0)

            def k_out_(g, par, e):
                left_over(g, e, 1, f"k{e}")

            def k_parts(g, par, e):
                last_part(g, e, 1)

            def relative(g, par, c):
                if c not in RQ_ON_SCALAR:
                    bank = rq_bank(c)
                    dve.wait_ge(full[bank], n_rel(g, bank, c) + 1)
                    vec.tensor_copy(rq3[:, :, RC * c:RC * (c + 1)],
                                    ps[bank][:, :].rearrange("p (m n) -> p n m", n=HB)).then_inc(empty[bank], 1)

            def logits(g, par, u):
                bank = 2 + u % 2
                if u == 0:
                    for n in (1, 3, 5):
                        dve.wait_ge(empty[n], g * USES[n] + RELATIVE_USES[n])
                dve.wait_ge(full[bank], n_logit(g, u) + 1)
                apart(dve)
                for b in range(GB):
                    n = GB * u + b
                    ins = vec.tensor_tensor_reduce(out=rq3[:, n, :], in0=ps[bank][:, b * S:(b + 1) * S],
                                                   in1=rq3[:, n, :], scale=1.0, scalar=LOWEST, op0=ALU.add,
                                                   op1=ALU.max, accum_out=mx[:, n:n + 1])
                ins.then_inc(empty[bank], 1)

            def turn_out(g, par, q):
                dve.wait_ge(full[1], n_pv(g, q) + 1)
                if q == 0 and past(g):
                    dve.wait_ge(o_sum, g)
                vec.tensor_copy(ot4[:, :, 4 * q:4 * q + 4, :],
                                ps[1][:, :].rearrange("p (b j c) -> p b j c", b=GB, j=4)[:, :, :, 0:VW])\
                   .then_inc(empty[1], 1)

            def combine(g, par):
                dve.wait_ge(empty[1], USES[1] * (g + 1))
                vec.reciprocal(rden[:, :], ot3[:, :, HD]).then_inc(rden_ready, 1)
                dve.wait_ge(orel_in, 16 * (g + 1))
                vec.tensor_tensor(h2[:, :].rearrange("p (b h d) -> p b h d", b=GB, d=HD), ot4[:, :, :, 0:HD],
                                  orel[:, :].rearrange("p (d h b) -> p b h d", d=HD, b=GB), ALU.add)\
                   .then_inc(o_sum, 1)
                dve.wait_ge(o_sum, g + 1)
                dve.wait_ge(rden_ready, g + 1)
                n3 = h2[:, :].rearrange("p (n d) -> p n d", d=HD)
                vec.tensor_tensor(n3, n3, rden[:, :].unsqueeze(2).broadcast_to([P, HB, HD]), ALU.mult)\
                   .then_inc(o_norm, 1)

            def stats2(g, par):
                dve.wait_ge(h2_ready, g + 1)
                statistics(2, g, h2)

            def apply2(g, par):
                normalise(2, g, h2, mrows)

            def mix_rows(g, dst, one_less):
                for c in range(CT):
                    dve.wait_ge(empty_m, n_mix(g, f"t{c}") + 1)
                    row = dst[:, c * TOK:(c + 1) * TOK].rearrange("p (b s) -> p b s", b=GB)
                    vec.scalar_tensor_tensor(row, nT[:, c * GB:(c + 1) * GB, 0:S], one_less[:, c:c + 1], row,
                                             ALU.mult, ALU.add).then_inc(mixed, 1)

            def mix_r(g, par):
                mix_rows(g, xr, omur)

            def mix_k(g, par):
                dve.wait_ge(k_scaled, CT * (g + 1))
                mix_rows(g, xk, omuk)

            def value_out(g, par, i):
                half = slice(TOK * i, TOK * (i + 1))
                dve.wait_ge(empty_m, n_mix(g, "r1") + 1)
                dve.wait_ge(full_m, n_mix(g, f"v{i}") + 1)
                vec.scalar_tensor_tensor(mrows[:, half], mrows[:, half], 1.0, ps[7][:, :], ALU.add, ALU.mult)\
                   .then_inc(empty_m, 1)
                dve.wait_ge(empty_m, n_mix(g, f"v{i}") + 1)
                vec.scalar_tensor_tensor(h2[:, half], mrows[:, half], 0.5, h2[:, half], ALU.mult, ALU.add)\
                   .then_inc(result, 1)

            steps = dict(type=type_, stats0=stats0, apply0=apply0, stats1=stats1, apply1=apply1,
                         q_out=q_out_, q_parts=q_parts,
                         k_out=k_out_, k_parts=k_parts, relative=relative, logits=logits, turn_out=turn_out,
                         combine=combine, stats2=stats2, apply2=apply2,
                         mix_r=mix_r, mix_k=mix_k, value_out=value_out)
            first_rows(steps)
            pipeline(dve, steps)

        @block.tensor
        def _(pe):
            mm = nc.tensor.matmul
            pe.wait_ge(const_in, N_CONST)
            pe.wait_ge(setup_v, 4 + 3)
            mm(ps[7][0:1, 0:TW], ones, prod, start=True, stop=True).then_inc(pp_sum, 1)
            pe.wait_ge(setup_g, N_SETUP_G)

            def transpose(dst, src, **kw):
                return mm(dst, src, ident[:, :], is_transpose=True, **kw)

            def features(dst, src, c):
                for b in range(GB):
                    ins = transpose(dst[:, b * S:(b + 1) * S], src[:, b * D + c * P:b * D + (c + 1) * P],
                                    start=True, stop=True)
                return ins

            def tile_product(dst, w, e, src):
                for c in range(CT):
                    ins = mm(dst[:, :], w[:, c * D + e * P:c * D + (e + 1) * P], src(c), start=c == 0, stop=c == CT - 1)
                return ins

            def row_product(dst, w, i, src):
                for n in range(2):
                    for c in range(CT):
                        ins = mm(dst[:, n * D:(n + 1) * D], src(c, 2 * i + n), w[:, c * D:(c + 1) * D],
                                 start=c == 0, stop=c == CT - 1)
                return ins

            def turn1(g, par, c):
                pe.wait_ge(normed[1], GB * (g + 1))
                if past(g) or c:
                    pe.wait_ge(empty_e, n_embed(g, f"t{c}"))
                features(ps[6], rows, c).then_inc(full_e, 1)

            def project(g, w, e, use):
                pe.wait_ge(empty_e, n_embed(g, use))
                tile_product(ps[6], w, e, lambda c: nT[:, c * GB:(c + 1) * GB, 1:S + 1]).then_inc(full_e, 1)

            def q(g, par, e):
                project(g, w_q, e, f"q{e}")

            def k(g, par, e):
                project(g, w_k, e, f"k{e}")

            def v(g, par, i):
                pe.wait_ge(empty_e, n_embed(g, f"v{i}"))
                row_product(ps[6], w_v, i, lambda c, b: nT[:, c * GB + b, 1:S + 1]).then_inc(full_e, 1)

            def relative(g, par, c):
                if c == 0 and not past(g):
                    pe.wait_ge(slots_in, 16 * (2 * SLOTS + NPART))
                if c == 0:
                    pe.wait_ge(q_in, 16 * SLOTS * (g + 1))
                    pe.wait_ge(k_in, 16 * SLOTS * (g + 1))
                bank = rk_bank(c)
                if past(g) or c > 2:
                    pe.wait_ge(empty[bank], n_rel(g, bank, c))
                for i in range(RC):
                    l = RC * c + i
                    ins = mm(ps[bank][:, i * HB:(i + 1) * HB], ekw[0:KR, S - 1 - l:TW - l], qs3[par][0:KR, :, l],
                             start=True, stop=True)
                ins.then_inc(full[bank], 1)
                bank = rq_bank(c)
                if past(g) or c > 2:
                    pe.wait_ge(empty[bank], n_rel(g, bank, c))
                for i in range(RC):
                    m = RC * c + i
                    ins = mm(ps[bank][:, i * HB:(i + 1) * HB], eqw[0:KR1, S - 1 - m:TW - m], ks3[par][0:KR1, :, m],
                             start=True, stop=True)
                ins.then_inc(full[bank], 1)

            def logits(g, par, u):
                bank = 2 + u % 2
                if u == 0:
                    for n in (0, 2, 4):
                        pe.wait_ge(empty[n], g * USES[n] + RELATIVE_USES[n])
                pe.wait_ge(empty[bank], n_logit(g, u))
                for b in range(GB):
                    n = GB * u + b
                    dst = ps[bank][:, b * S:(b + 1) * S]
                    mm(dst, qs3[par][0:KR, n, :], ks3[par][0:KR, n, :], start=True, stop=False)
                    ins = transpose(dst, rk3[:, n, :], start=False, stop=True)
                ins.then_inc(full[bank], 1)

            def probT(g, par, u):
                bank = 4 + u % 2
                pe.wait_ge(exp_done, H // 2 * g + u // 2 + 1)
                pe.wait_ge(empty[bank], n_probT(g, u))
                for b in range(GB):
                    ins = transpose(ps[bank][:, b * S:(b + 1) * S], rq3[:, GB * u + b, :], start=True, stop=True)
                ins.then_inc(full[bank], 1)

            def weigh(g, par, q):
                for n in (4, 5):
                    pe.wait_ge(empty[n], n_probT(g, 4 * q + 4))
                pe.wait_ge(empty[0], n_pv(g, q))
                if q == 0:
                    pe.wait_ge(empty_e, n_embed(g, "v1") + 1)
                for b in range(GB):
                    for j in range(4):
                        hd = 4 * q + j
                        ins = mm(ps[0][32 * j:32 * j + VW, b * S:(b + 1) * S], vx4[:, b, hd, :],
                                 rk3[:, GB * hd + b, :], start=True, stop=True, tile_position=(0, 32 * j))
                ins.then_inc(full[0], 1)

            def turn(g, par, q):
                pe.wait_ge(empty[0], n_pv(g, q) + 1)
                pe.wait_ge(empty[1], n_pv(g, q))
                for b in range(GB):
                    ins = transpose(ps[1][:, b * P:(b + 1) * P], pv[:, b * S:(b + 1) * S], start=True, stop=True)
                ins.then_inc(full[1], 1)

            def weigh_rel(g, par, c):
                bank = AV_BANK[c]
                pe.wait_ge(empty[bank], n_av(g, c))
                for i in range(8):
                    for j in range(4):
                        l = 32 * j + 8 * c + i
                        ins = mm(ps[bank][32 * j:32 * j + HD, i * HB:(i + 1) * HB], avt[:, (S - 1 - l) * HD:(S - l) * HD],
                                 rk3[:, :, l], start=True, stop=True, tile_position=(0, 32 * j))
                ins.then_inc(full[bank], 1)

            def turn2(g, par, c):
                pe.wait_ge(normed[2], GB * (g + 1))
                if isinstance(g, int) or c:
                    pe.wait_ge(empty_m, n_mix(g, f"t{c}"))
                features(ps[7], mrows, c).then_inc(full_m, 1)

            def gate(g, par, i):
                pe.wait_ge(mixed, 2 * CT * g + CT)
                pe.wait_ge(empty_m, n_mix(g, f"r{i}"))
                row_product(ps[7], w_r, i, lambda c, b: xr[:, c * TOK + b * S:c * TOK + (b + 1) * S])\
                    .then_inc(full_m, 1)

            def key(g, par, e):
                pe.wait_ge(mixed, 2 * CT * (g + 1))
                pe.wait_ge(empty_m, n_mix(g, f"k{e}"))
                tile_product(ps[7], w_fk, e, lambda c: xk[:, c * TOK:(c + 1) * TOK]).then_inc(full_m, 1)

            def value(g, par, i):
                pe.wait_ge(squared, CT * (g + 1))
                pe.wait_ge(empty_m, n_mix(g, f"v{i}"))
                row_product(ps[7], w_fv, i, lambda c, b: kact[:, c * TOK + b * S:c * TOK + (b + 1) * S])\
                    .then_inc(full_m, 1)

            steps = dict(turn1=turn1, q=q, k=k, v=v, relative=relative, logits=logits, probT=probT,
                         weigh=weigh, turn=turn, weigh_rel=weigh_rel, turn2=turn2, gate=gate, key=key,
                         value=value)
            first_rows(steps)
            pipeline(pe, steps)


_INS = ['ids', 'types', 'word', 'pos', 'typ', 'gamma', 'beta', 'wq', 'wk', 'wv', 'eq', 'ek', 'ev',
        'wr_t', 'wk_t', 'wv_t', 'mu_r', 'mu_k']


def kernel(**inputs):
    import numpy as np
    import concourse.bacc as bacc
    from concourse.bass_utils import run_bass_kernel_spmd

    x = {k: np.asarray(v) for k, v in inputs.items()}

    def by_group(a):
        return a.reshape(NG, GB, S).transpose(0, 2, 1)

    data = dict(
        ids=by_group(x['x']), types=by_group(x['mask_BS_i1_0']), word=x['L0_tok_word_emb'],
        pos=x['L0_tok_pos_emb'], typ=x['L0_tok_type_emb'], gamma=x['L0_tok_gamma'], beta=x['L0_tok_beta'],
        wq=x['L0_attn_Wq'], wk=x['L0_attn_Wk'], wv=x['L0_attn_Wv'], eq=x['L0_attn_Eq'].T, ek=x['L0_attn_Ek'].T,
        ev=x['L0_attn_Ev'][::-1], wr_t=x['L0_ffn_W_r'].T, wk_t=x['L0_ffn_W_k'].T, wv_t=x['L0_ffn_W_v'].T,
        mu_r=x['L0_ffn_mu_r'].reshape(CT, P).T, mu_k=x['L0_ffn_mu_k'].reshape(CT, P).T)
    nc = bacc.Bacc("TRN2", target_bir_lowering=False, num_devices=1, dynamic_dma_scratch_size=8192)
    arrays, args = {}, []
    for name in _INS:
        a = np.ascontiguousarray(data[name])
        arrays[f"in_{name}"] = a
        args.append(nc.dram_tensor(f"in_{name}", a.shape, mybir.dt.from_np(a.dtype), kind="ExternalInput").ap())
    out = nc.dram_tensor("out", (B, S, D), fp32, kind="ExternalOutput").ap()
    tower_kernel(nc, *args, out.rearrange("(g b) s n -> g s b n", b=GB))
    r = run_bass_kernel_spmd(nc, [arrays], core_ids=[0])
    return r.results[0]["out"]
```
